# Optimizing a Trainium2 kernel written in Bass

```python
import numpy as np
import jax
import jax.numpy as jnp

def _softmax(x, axis=-1):
    return jax.nn.softmax(x, axis=axis)

def _gelu(x):
    return jax.nn.gelu(x, approximate=True)

def _silu(x):
    return jax.nn.silu(x)

def _sigmoid(x):
    return jax.nn.sigmoid(x)

def _layernorm(x, axis=-1, eps=1e-05):
    m = jnp.mean(x, axis=axis, keepdims=True)
    v = jnp.var(x, axis=axis, keepdims=True)
    return (x - m) / jnp.sqrt(v + eps)

def _scatter_add(tgt, idx, src, axis=0):
    return tgt.at[idx].add(src)

def _segment_sum(src, seg, n):
    return jax.ops.segment_sum(src, seg, n)
kernel_name = 'mk_adj_preln_d4_adj_r2_546b9a'

def setup_inputs(seed: int=0):
    np.random.seed(seed)
    _w = jnp.asarray

    def _rec_inputs():
        import jax
        import jax.numpy as jnp
        _gk = jax.random.key(seed)
        x = -0.0005207 + 1.001 * jax.random.normal(jax.random.fold_in(_gk, 1), (8, 1024, 128), jnp.float32)
        _a = jax.random.bernoulli(jax.random.fold_in(_gk, 2), 0.00195312, (1024, 1024))
        _a = jnp.logical_or(_a, jnp.swapaxes(_a, -1, -2))
        _a = jnp.logical_or(_a, jnp.eye(1024, dtype=bool))
        _af = _a.astype(jnp.float32)
        _af = _af * jax.random.uniform(jax.random.fold_in(_gk, 3), (1024, 1024), jnp.float32, 0.05, 1)
        adj = _af
        return (x, adj)
    x, adj = _rec_inputs()

    def _L0_gnn_setup():
        import jax, jax.numpy as jnp
        import numpy as np
        B, N, C_IN, C_OUT = (8, 1024, 128, 128)
        key = jax.random.key(seed)
        k1, k2, k3 = jax.random.split(key, 3)
        x = jax.random.normal(k1, (B, N, C_IN), dtype=jnp.float32)
        adj = jax.random.uniform(k2, (N, N), dtype=jnp.float32)
        W = jax.random.normal(k3, (C_OUT, C_IN), dtype=jnp.float32) * (1.0 / np.sqrt(C_IN))
        b = jnp.zeros((C_OUT,), dtype=jnp.float32)
        return {'x': x, 'adj': adj, 'W': W, 'b': b}
    _L0_gnn_all = _L0_gnn_setup()
    _L0_gnn_in = {k: v for k, v in _L0_gnn_all.items() if k in ('W', 'b')}
    del _L0_gnn_all

    def _L1_gnn_setup():
        import jax, jax.numpy as jnp
        import numpy as np
        B, N, F_IN, F_OUT = (4, 2048, 128, 128)
        NEG_SLOPE = 0.2
        EDGE_PROB = 0.05
        key = jax.random.key(seed)
        kx, ka, kw, ks, kd = jax.random.split(key, 5)
        x = jax.random.normal(kx, (B, N, F_IN), dtype=jnp.float32)
        a = (jax.random.uniform(ka, (N, N)) < EDGE_PROB).astype(jnp.float32)
        a = a.at[jnp.arange(N), jnp.arange(N)].set(1.0)
        bw = float(np.sqrt(6.0 / (F_IN + F_OUT)))
        w = jax.random.uniform(kw, (F_IN, F_OUT), minval=-bw, maxval=bw, dtype=jnp.float32)
        ba = float(np.sqrt(6.0 / (1 + F_OUT)))
        a_src = jax.random.uniform(ks, (F_OUT,), minval=-ba, maxval=ba, dtype=jnp.float32)
        a_dst = jax.random.uniform(kd, (F_OUT,), minval=-ba, maxval=ba, dtype=jnp.float32)
        return {'x': x, 'a': a, 'w': w, 'a_src': a_src, 'a_dst': a_dst}
    _L1_gnn_all = _L1_gnn_setup()
    _L1_gnn_in = {k: v for k, v in _L1_gnn_all.items() if k in ('w', 'a_src', 'a_dst')}
    del _L1_gnn_all

    def _L2_gnn_setup():
        import jax, jax.numpy as jnp
        import numpy as np
        B, N, D, OUT = (8, 1024, 128, 128)
        key = jax.random.key(seed)
        k1, k2, k3, k4, k5, k6 = jax.random.split(key, 6)
        stdv = 1.0 / np.sqrt(OUT)
        inputs = jax.random.normal(k1, (B, N, D), dtype=jnp.float32)
        relation = jax.random.normal(k2, (N, N), dtype=jnp.float32)
        gl = 1.0 / np.sqrt(2 * D + 1)
        g_w = jax.random.uniform(k3, (2 * D + 1,), minval=-gl, maxval=gl, dtype=jnp.float32)
        g_b = jax.random.uniform(k4, (), minval=-gl, maxval=gl, dtype=jnp.float32)
        weight = jax.random.uniform(k5, (D, OUT), minval=-stdv, maxval=stdv, dtype=jnp.float32)
        bias = jax.random.uniform(k6, (OUT,), minval=-stdv, maxval=stdv, dtype=jnp.float32)
        return {'inputs': inputs, 'relation': relation, 'g_w': g_w, 'g_b': g_b, 'weight': weight, 'bias': bias}
    _L2_gnn_all = _L2_gnn_setup()
    _L2_gnn_in = {k: v for k, v in _L2_gnn_all.items() if k in ('g_w', 'g_b', 'weight', 'bias')}
    del _L2_gnn_all

    def _L3_gnn_setup():
        import jax, jax.numpy as jnp
        import numpy as np
        from jax import lax
        CONV_ORDER = 3

        def _chebyshev(adj, x, order):

            def step(carry, _):
                nxt = jnp.einsum('ij,bjc->bic', adj, carry)
                return (nxt, nxt)
            _, xs = lax.scan(step, x, None, length=order)
            return jnp.moveaxis(xs, 0, -1)
        key = jax.random.key(seed)
        k1, k2, k3, k4 = jax.random.split(key, 4)
        B, E, C_in, C_out, K, n_adjs = (8, 2048, 128, 128, CONV_ORDER, 2)
        x_1 = jax.random.normal(k1, (B, E, C_in), dtype=jnp.float32)
        adj0 = jax.random.normal(k2, (E, E), dtype=jnp.float32) / np.sqrt(E)
        adj1 = jax.random.normal(k3, (E, E), dtype=jnp.float32) / np.sqrt(E)
        kdim = K * n_adjs + 1
        std = 1.414 * np.sqrt(2.0 / float((C_in + C_out) * kdim))
        weight_1 = std * jax.random.normal(k4, (C_in, C_out, kdim), dtype=jnp.float32)
        return {'x_1': x_1, 'adj0': adj0, 'adj1': adj1, 'weight_1': weight_1}
    _L3_gnn_all = _L3_gnn_setup()
    _L3_gnn_in = {k: v for k, v in _L3_gnn_all.items() if k in ('weight_1',)}
    del _L3_gnn_all
    return {'x': x, 'adj': adj, 'L0_gnn_W': _L0_gnn_in['W'], 'L0_gnn_b': _L0_gnn_in['b'], 'L1_gnn_w': _L1_gnn_in['w'], 'L1_gnn_a_src': _L1_gnn_in['a_src'], 'L1_gnn_a_dst': _L1_gnn_in['a_dst'], 'L2_gnn_g_w': _L2_gnn_in['g_w'], 'L2_gnn_g_b': _L2_gnn_in['g_b'], 'L2_gnn_weight': _L2_gnn_in['weight'], 'L2_gnn_bias': _L2_gnn_in['bias'], 'L3_gnn_weight_1': _L3_gnn_in['weight_1']}

def reference(x, adj, L0_gnn_W, L0_gnn_b, L1_gnn_w, L1_gnn_a_src, L1_gnn_a_dst, L2_gnn_g_w, L2_gnn_g_b, L2_gnn_weight, L2_gnn_bias, L3_gnn_weight_1):
    import jax
    import jax.numpy as jnp

    def _L0_gnn_ref(x, adj, W, b):
        import jax, jax.numpy as jnp
        import numpy as np
        B, N, C_IN, C_OUT = (8, 1024, 128, 128)
        n = x.shape[1]
        A_hat = adj + jnp.eye(n, dtype=adj.dtype)
        d = jnp.sum(A_hat, axis=-1) ** (-0.5)
        A_norm = d[:, None] * A_hat * d[None, :]
        out = jnp.einsum('nm,bmc->bnc', A_norm, x)
        out = jnp.einsum('bnc,oc->bno', out, W) + b
        return out

    def _L1_gnn_ref(x, a, w, a_src, a_dst):
        import jax, jax.numpy as jnp
        import numpy as np
        B, N, F_IN, F_OUT = (4, 2048, 128, 128)
        NEG_SLOPE = 0.2
        EDGE_PROB = 0.05
        h = jnp.einsum('bnf,fo->bno', x, w)
        e_src = jnp.einsum('bno,o->bn', h, a_src)
        e_dst = jnp.einsum('bno,o->bn', h, a_dst)
        e = jax.nn.leaky_relu(e_src[:, :, None] + e_dst[:, None, :], negative_slope=NEG_SLOPE)
        mask = (a > 0)[None, :, :]
        e = jnp.where(mask, e, -jnp.inf)
        alpha = jax.nn.softmax(e, axis=-1)
        out = jnp.einsum('bij,bjo->bio', alpha, h)
        return out

    def _L2_gnn_ref(inputs, relation, g_w, g_b, weight, bias):
        import jax, jax.numpy as jnp
        import numpy as np
        B, N, D, OUT = (8, 1024, 128, 128)
        b, n, d = inputs.shape
        w_j = g_w[:d]
        w_i = g_w[d:2 * d]
        w_r = g_w[2 * d]
        sj = inputs @ w_j
        si = inputs @ w_i
        res = si[:, :, None] + sj[:, None, :] + relation[None] * w_r + g_b
        agg = jnp.einsum('bij,bjd->bid', res, inputs)
        return agg @ weight + bias

    def _L3_gnn_ref(x_1, adj0, adj1, weight_1):
        import jax, jax.numpy as jnp
        import numpy as np
        from jax import lax
        CONV_ORDER = 3

        def _chebyshev(adj, x, order):

            def step(carry, _):
                nxt = jnp.einsum('ij,bjc->bic', adj, carry)
                return (nxt, nxt)
            _, xs = lax.scan(step, x, None, length=order)
            return jnp.moveaxis(xs, 0, -1)
        parts = [x_1[..., None], _chebyshev(adj0, x_1, CONV_ORDER), _chebyshev(adj1, x_1, CONV_ORDER)]
        x_all = jnp.concatenate(parts, axis=3)
        y_1 = jnp.einsum('bnik,iok->bno', x_all, weight_1)
        return y_1
    h = jnp.maximum(_layernorm(x, axis=-1), 0.0)
    x = x + _L0_gnn_ref(h, adj, L0_gnn_W, L0_gnn_b)
    h = jnp.maximum(_layernorm(x, axis=-1), 0.0)
    x = x + _L1_gnn_ref(h, adj, L1_gnn_w, L1_gnn_a_src, L1_gnn_a_dst)
    h = jnp.maximum(_layernorm(x, axis=-1), 0.0)
    x = x + _L2_gnn_ref(h, adj, L2_gnn_g_w, L2_gnn_g_b, L2_gnn_weight, L2_gnn_bias)
    h = jnp.maximum(_layernorm(x, axis=-1), 0.0)
    x = x + _L3_gnn_ref(h, adj, adj, L3_gnn_weight_1)
    return x

_drawn_inputs = setup_inputs


def setup_inputs(seed=0):
    import zlib

    import numpy as np

    out = dict(_drawn_inputs(seed))
    spreads = {'L0_gnn_b': (0.0, 0.1)}
    factors = {'L2_gnn_bias': 55.886}
    for name, (base, spread) in spreads.items():
        noise = np.random.default_rng([zlib.crc32(name.encode()), seed]).standard_normal(out[name].shape)
        drawn = base * np.exp(spread * noise) if base else spread * noise
        out[name] = jnp.asarray(drawn.astype(out[name].dtype))
    for name, factor in factors.items():
        out[name] = (out[name] * factor).astype(out[name].dtype)
    return out
```

```python
import concourse.bass as bass
from concourse import mybir
from contextlib import ExitStack

B, N, C = 8, 1024, 128
P = 128
T = N // P
HALF = N // 2
HT = T // 2
PAIRS = T // 2
EPS = 1e-5
SLOPE = 0.2
MASKED = -3.0e38
KDIM = 7
GROUP = 4
STAGES = 3

SIDE_STEPS = [("hT0", 1), ("hT1", 1), ("h1_0", 1), ("h1_1", 1), ("L0p0", 2),
              ("BT0", -1), ("BT1", -1), ("L0p1", 2), ("D0", 1), ("D1", 1),
              ("L0w0", 2), ("L0w1", 2), ("L2p0", -1), ("L2p1", -1), ("L2w0", -1), ("L2w1", -1)]
OFFSET = dict(SIDE_STEPS)
PROLOGUE = [("L0p0", 0), ("L0p1", 0), ("L0w0", 0), ("L0w1", 0),
            ("hT0", 0), ("hT1", 0), ("h1_0", 0), ("h1_1", 0), ("D0", 0), ("D1", 0),
            ("L0p0", 1), ("L0p1", 1), ("L0w0", 1), ("L0w1", 1)]
SIDE_ORDER = PROLOGUE + [(s, t + o) for t in range(B + 1) for s, o in SIDE_STEPS if 0 <= t + o < B]
SIDE_INDEX = {}
for _n, _key in enumerate(SIDE_ORDER):
    SIDE_INDEX.setdefault(_key, _n)
LOOP_FROM, LOOP_TO = 2, 5


def known(v):
    return isinstance(v, int)


def exists(b):
    return not known(b) or 0 <= b < B


def side(step, b):
    if known(b):
        return SIDE_INDEX[step, b] % 2, SIDE_INDEX[step, b] // 2
    first = OFFSET[step] + LOOP_FROM
    n = SIDE_INDEX[step, first]
    assert all(SIDE_INDEX[step, first + k] == n + k * len(SIDE_STEPS) for k in range(LOOP_TO - LOOP_FROM))
    return n % 2, (b - first) * (len(SIDE_STEPS) // 2) + n // 2


def wait(eng, sem, value):
    if not known(value) or value > 0:
        eng.wait_ge(sem, value)


def build(nc, x, adj, W0, b0, w1, a_src, a_dst, g_w, g_b, W2, bias2, W3, out):
    f32, f32r, bf16 = mybir.dt.float32, mybir.dt.float32r, mybir.dt.bfloat16
    ALU, ACT = mybir.AluOpType, mybir.ActivationFunctionType
    ctx = ExitStack()
    with ctx:
        x1_dram = nc.dram_tensor("x1_scratch", (B, P, N), f32, kind="Internal").ap()
        x3_dram = nc.dram_tensor("x3_scratch", (B, P, N), f32, kind="Internal").ap()

        def sem(name):
            return ctx.enter_context(nc.semaphore(name))

        def keep(name, shape, dt=f32):
            return ctx.enter_context(nc.sbuf_tensor(name, shape, dt))

        at_hi = keep("at_hi", [P, T, N], f32r)
        at_lo = keep("at_lo", [P, T, N], f32r)
        ident = keep("ident", [P, P])
        neg_half = keep("neg_half", [P, T])

        phase1 = ExitStack()

        def sb(name, shape, dt=f32):
            return phase1.enter_context(nc.sbuf_tensor(name, shape, dt))

        with ExitStack() as setup:
            a_nat = setup.enter_context(nc.sbuf_tensor("a_nat", [P, T, N], f32))
        pt_hi = sb("pt_hi", [P, 2, T, 2 * P], f32r)
        pt_lo = sb("pt_lo", [P, 2, T, 2 * P], f32r)
        mask = sb("mask", [P, T, N], bf16)
        tm = sb("tm", [P, 4, N])
        e2 = sb("e2", [P, 2, N])
        d_row = sb("d_row", [P, N])
        xc = sb("xc", [P, T, C])
        xa = sb("xa", [P, T, C])
        xb = sb("xb", [P, T, C])
        hn = sb("hn", [P, T, C])
        g_hi = sb("g_hi", [P, T, C], f32r)
        g_lo = sb("g_lo", [P, T, C], f32r)
        u_hi = sb("u_hi", [P, N], f32r)
        u_lo = sb("u_lo", [P, N], f32r)
        h1s = sb("h1s", [P, N])
        h1_hi = sb("h1_hi", [P, N], f32r)
        h1_lo = sb("h1_lo", [P, N], f32r)
        ot_hi = sb("ot_hi", [P, N], f32r)
        ot_lo = sb("ot_lo", [P, N], f32r)
        avt = sb("avt", [P, N])
        w0t_hi = sb("w0t_hi", [P, C], f32r)
        w0t_lo = sb("w0t_lo", [P, C], f32r)
        w1_hi = sb("w1_hi", [P, C], f32r)
        w1_lo = sb("w1_lo", [P, C], f32r)
        wa_hi = sb("wa_hi", [P, 2], f32r)
        wa_lo = sb("wa_lo", [P, 2], f32r)
        w2 = sb("w2", [P, C])
        w2r_hi = sb("w2r_hi", [P, C], f32r)
        w2r_lo = sb("w2r_lo", [P, C], f32r)
        ident_r = sb("ident_r", [P, P], f32r)
        b0_row = sb("b0_row", [P, C])
        bias2_row = sb("bias2_row", [P, C])
        gw_row = sb("gw_row", [P, 2 * C + 1])
        gb_col = sb("gb_col", [P, 1])
        hw_row = sb("hw_row", [P, 2, C])
        c_row = sb("c_row", [P, C])
        wait_cell = sb("wait_cell", [P, 4])
        junk = sb("junk", [P, 2, C])
        dm = sb("dm", [P, T])
        s_col = sb("s_col", [P, T])
        b1 = sb("b1", [P, T])
        b2 = sb("b2", [P, T])
        ct = sb("ct", [P, 5, T])
        slopes = sb("slopes", [P, T])
        rsum = sb("rsum", [P, T])
        rinv = sb("rinv", [P, T])
        sji = sb("sji", [P, 2, T])
        sv_a = sb("sv_a", [P, T, 2], f32r)
        sv_b = sb("sv_b", [P, T, 2], f32r)
        hg = sb("hg", [P, 3])
        d_raw = sb("d_raw", [P, T])
        d_col = sb("d_col", [P, T])
        st = [sb(f"st{k}", [P, T, 6]) for k in range(3)]
        lt = [sb(f"lt{k}", [P, 8, T]) for k in range(3)]
        rstd = [sb(f"rstd{k}", [P, T]) for k in range(3)]
        nb = [sb(f"nb{k}", [P, T]) for k in range(3)]
        w_stage = tm[:, 0, :].rearrange("p (k c) -> p k c", c=C)
        wa_stage = tm[:, 1, 0:2]
        phase1.close()

        phase2 = ExitStack()

        def sb2(name, shape, dt=f32):
            return phase2.enter_context(nc.sbuf_tensor(name, shape, dt))

        xg = sb2("xg", [P, GROUP, T, C])
        v = [sb2(f"v{k}", [P, T, GROUP, C]) for k in (2, 1)]
        uu_hi = [sb2(f"uu_hi{k}", [P, T, GROUP * C], f32r) for k in range(2)]
        uu_lo = [sb2(f"uu_lo{k}", [P, T, GROUP * C], f32r) for k in range(2)]
        h3 = sb2("h3", [P, T, C])
        ht_hi = sb2("ht_hi", [P, N], f32r)
        ht_lo = sb2("ht_lo", [P, N], f32r)
        w3_raw = sb2("w3_raw", [P, C, KDIM])
        w3_sum = sb2("w3_sum", [P, 4, C])
        w3_hi = sb2("w3_hi", [P, 4 * C], f32r)
        w3_lo = sb2("w3_lo", [P, 4 * C], f32r)
        st3 = sb2("st3", [P, T, 6])
        lt3 = sb2("lt3", [P, 8, T])
        rstd3 = sb2("rstd3", [P, T])
        nb3 = sb2("nb3", [P, T])
        phase2.close()

        tr = [ctx.enter_context(nc.psum_tensor(f"tr{k}", [P, N], f32)) for k in range(2)]
        pv_bank = ctx.enter_context(nc.psum_tensor("pv_bank", [P, HALF], f32))
        misc = ctx.enter_context(nc.psum_tensor("misc", [P, HALF], f32))
        side_bank = [ctx.enter_context(nc.psum_tensor(f"side{k}", [P, HALF], f32)) for k in range(2)]
        ring = [tr[0][:, 0:HALF], tr[0][:, HALF:N], tr[1][:, 0:HALF], tr[1][:, HALF:N]]

        adj_in = [sem(f"adj_in{k}") for k in range(4)]
        w_in, x_in = sem("w_in"), sem("x_in")
        ident_done, mask_done, rows_summed = sem("ident_done"), sem("mask_done"), sem("rows_summed")
        at_tr, at_hi_done, at_lo_done = sem("at_tr"), sem("at_hi_done"), sem("at_lo_done")
        w0_tr, w0_hi_done = sem("w0_tr"), sem("w0_hi_done")
        w_ready, w_ready_dve, d_step = sem("w_ready"), sem("w_ready_dve"), sem("d_step")
        side_full = [sem(f"side_full{k}") for k in range(2)]
        side_free = [sem(f"side_free{k}") for k in range(2)]
        x1_stored, x1_loaded, x3_stored = sem("x1_stored"), sem("x1_loaded"), sem("x3_stored")
        stats = [sem(f"stats{k}") for k in range(3)]
        ln_step = [sem(f"ln_step{k}") for k in range(3)]
        h_ready = [sem(f"h_ready{k}") for k in range(3)]
        g_hi_done, g_lo_done, xc_biased = sem("g_hi_done"), sem("g_lo_done"), sem("xc_biased")
        o0_hi, o2_hi, t_hi = sem("o0_hi"), sem("o2_hi"), sem("t_hi")
        h1_hi_done, h1_lo_done = sem("h1_hi_done"), sem("h1_lo_done")
        s_full, s_ready = sem("s_full"), sem("s_ready")
        scored, coef_step, exps = sem("scored"), sem("coef_step"), sem("exps")
        e2_done = sem("e2_done")
        p_max, p_tr, p_hi, p_lo = sem("p_max"), sem("p_tr"), sem("p_hi"), sem("p_lo")
        pv_done, av_read, rinv_done = sem("pv_done"), sem("av_read"), sem("rinv_done")
        u2_hi, u2_lo = sem("u2_hi"), sem("u2_lo")
        sji_step, sv_done = sem("sji_step"), sem("sv_done")
        moments_done, hg_step, hw_full, hw_read = sem("moments_done"), sem("hg_step"), sem("hw_full"), sem("hw_read")
        xb_biased, hw_added = sem("xb_biased"), sem("hw_added")

        def filled(step, b):
            k, n = side(step, b)
            return side_full[k], n + 1

        def drained(step, b):
            k, n = side(step, b)
            return side_free[k], n + 1

        LN_STEPS = [11, 10, 10]
        PAIR_STEPS = 7
        COEF_STEPS = PAIR_STEPS * PAIRS

        def norm_coefficients(eng, s, l, rs, n_b, stats_sem, have, step_sem, base, scale_col):
            wait(eng, stats_sem, have)
            wait(eng, step_sem, base)
            total, delta, square, var, part, sum_v, neg_mean = (l[:, k, :] for k in range(7))
            nc.gpsimd.tensor_tensor(total, s[:, :, 1], s[:, :, 4], ALU.add).then_inc(step_sem, 1)
            nc.gpsimd.tensor_tensor(delta, s[:, :, 1], s[:, :, 4], ALU.subtract).then_inc(step_sem, 1)
            nc.gpsimd.tensor_tensor(square, s[:, :, 2], s[:, :, 5], ALU.add).then_inc(step_sem, 1)
            eng.wait_ge(step_sem, base + 3)
            nc.gpsimd.tensor_tensor(part, delta, neg_half[:, :], ALU.mult).then_inc(step_sem, 1)
            nc.gpsimd.tensor_scalar(var, square, 1.0 / C, EPS, ALU.mult, ALU.add).then_inc(step_sem, 1)
            nc.gpsimd.tensor_tensor(neg_mean, total, neg_half[:, :], ALU.mult).then_inc(step_sem, 1)
            eng.wait_ge(step_sem, base + 4)
            nc.gpsimd.tensor_tensor(delta, part, part, ALU.mult).then_inc(step_sem, 1)
            eng.wait_ge(step_sem, base + 7)
            nc.gpsimd.tensor_tensor(sum_v, var, delta, ALU.add).then_inc(step_sem, 1)
            eng.wait_ge(step_sem, base + 8)
            if scale_col is None:
                nc.gpsimd.tensor_tensor(rs, sum_v, neg_half[:, :], ALU.pow).then_inc(step_sem, 1)
                eng.wait_ge(step_sem, base + 9)
            else:
                nc.gpsimd.tensor_tensor(part, sum_v, neg_half[:, :], ALU.pow).then_inc(step_sem, 1)
                eng.wait_ge(step_sem, base + 9)
                nc.gpsimd.tensor_tensor(rs, part, scale_col, ALU.mult).then_inc(step_sem, 1)
                eng.wait_ge(step_sem, base + 10)
            nc.gpsimd.tensor_tensor(n_b, neg_mean, rs, ALU.mult).then_inc(step_sem, 1)

        w3_in, w3_step = sem("w3_in"), sem("w3_step")
        xg_in = [sem(f"xg_in{k}") for k in range(GROUP)]
        stats3, ln3_step, h3_ready = sem("stats3"), sem("ln3_step"), sem("h3_ready")
        ht_full, ht_hi_done, ht_lo_done = sem("ht_full"), sem("ht_hi_done"), sem("ht_lo_done")
        ring_full, ring_free = sem("ring_full"), sem("ring_free")
        v_hi, v_copied, v_read = sem("v_hi"), sem("v_copied"), sem("v_read")
        stage_sum, stage_hi, stage_lo = sem("stage_sum"), sem("stage_hi"), sem("stage_lo")
        out_stored = sem("out_stored")
        V_STEPS = GROUP * T
        S_STEPS = STAGES * T
        RING_STEPS = V_STEPS + S_STEPS

        block = ctx.enter_context(nc.Block())

        @block.sync
        def _(sp):
            sp.dma_start(xc[:, :, :], x[0].rearrange("(k p) c -> p k c", p=P)).then_inc(x_in, 16)
            for k in range(4):
                sp.dma_start(a_nat[:, 2 * k:2 * k + 2, :],
                             adj[2 * k * P:(2 * k + 2) * P, :].rearrange("(k p) n -> p k n", p=P)
                             ).then_inc(adj_in[k], 16)

            def load_x(b):
                wait(sp, *drained("L0w1", b - 1))
                sp.dma_start(xc[:, :, :], x[b:b + 1].rearrange("o (k p) c -> p (o k) c", p=P)
                             if known(b) else
                             x[bass.ds(b, 1)].rearrange("o (k p) c -> p (o k) c", p=P)).then_inc(x_in, 16)

            def one(dram, b):
                return (dram[b:b + 1] if known(b) else dram[bass.ds(b, 1)]).rearrange("o p n -> p (o n)")

            def store_x1(b):
                wait(sp, *drained("L0w1", b))
                sp.dma_start(one(x1_dram, b), xa[:, :, :].rearrange("p k c -> p (k c)")).then_inc(x1_stored, 16)

            def load_x1(b):
                wait(sp, x3_stored, 16 * b)
                wait(sp, x1_stored, 16 * (b + 1))
                sp.dma_start(xb[:, :, :].rearrange("p k c -> p (k c)"), one(x1_dram, b)).then_inc(x1_loaded, 16)

            def store_x3(b):
                wait(sp, *drained("L2w1", b))
                sp.dma_start(one(x3_dram, b), xb[:, :, :].rearrange("p k c -> p (k c)")).then_inc(x3_stored, 16)

            def iteration(t):
                if exists(t + 2):
                    store_x1(t + 2)
                if exists(t + 3):
                    load_x(t + 3)
                if exists(t - 1):
                    store_x3(t - 1)
                if exists(t):
                    load_x1(t)

            store_x1(0)
            load_x(1)
            store_x1(1)
            load_x(2)
            for t in range(0, LOOP_FROM):
                iteration(t)
            with sp.Fori(LOOP_FROM, LOOP_TO) as t:
                iteration(t)
            for t in range(LOOP_TO, B + 1):
                iteration(t)

            sp.wait_ge(x3_stored, 16 * B)
            sp.dma_start(w3_raw[:, :, :], W3).then_inc(w3_in, 16)
            for g in range(B // GROUP):
                wait(sp, out_stored, g * (16 * T))
                for b in range(GROUP):
                    sp.dma_start(xg[:, b].rearrange("p k c -> p (k c)"),
                                 x3_dram[bass.ds(g * GROUP + b, 1)].rearrange("o p n -> p (o n)")
                                 ).then_inc(xg_in[b], 16)
                for i in range(T):
                    wait(sp, stage_sum, g * S_STEPS + 2 * T + i + 1)
                    sp.dma_start(out[bass.ds(g * GROUP, GROUP), i * P:(i + 1) * P, :].rearrange("b p c -> p b c"),
                                 xg[:, :, i, :]).then_inc(out_stored, 16)
            wait(sp, out_stored, (B // GROUP) * 16 * T)

        @block.gpsimd
        def _(pool):
            nc.gpsimd.memset(ident[:, :], 0.0).then_inc(ident_done, 1)
            nc.gpsimd.memset(neg_half[:, :], -0.5)
            nc.gpsimd.memset(slopes[:, :], SLOPE)
            pool.wait_ge(ident_done, 1)
            nc.gpsimd.affine_select(out=ident[:, :], in_=ident[:, :], compare_op=ALU.not_equal, fill=1.0,
                                    base=0, pattern=[[-1, P]], channel_multiplier=1).then_inc(ident_done, 1)
            pool.wait_ge(rows_summed, T)
            pool.wait_ge(ident_done, 2)
            nc.gpsimd.tensor_scalar(d_raw[:, :], d_raw[:, :], 1.0, None, ALU.add).then_inc(d_step, 1)
            pool.wait_ge(d_step, 1)
            nc.gpsimd.tensor_tensor(d_col[:, :], d_raw[:, :], neg_half[:, :], ALU.pow).then_inc(d_step, 1)
            pool.wait_ge(d_step, 2)

            def coefficients(L, b):
                wait(pool, h_ready[L], b)
                norm_coefficients(pool, st[L], lt[L], rstd[L][:, :], nb[L][:, :], stats[L], b + 1,
                                  ln_step[L], LN_STEPS[L] * b, d_col[:, :] if L == 0 else None)

            def g_low(b):
                wait(pool, g_hi_done, b + 1)
                if exists(b - 1):
                    wait(pool, *filled("L0p1", b - 1))
                nc.gpsimd.tensor_tensor(g_lo[:, :, :], hn[:, :, :], g_hi[:, :, :].bitcast(f32),
                                        ALU.subtract).then_inc(g_lo_done, 1)

            def bias_xc(b):
                wait(pool, h_ready[0], b + 1)
                nc.gpsimd.tensor_tensor(xc[:, :, :], xc[:, :, :],
                                        b0_row[:, :].unsqueeze(1).broadcast_to([P, T, C]),
                                        ALU.add).then_inc(xc_biased, 1)

            def h1_low(b):
                wait(pool, h1_hi_done, b + 1)
                nc.gpsimd.tensor_tensor(h1_lo[:, :], h1s[:, :], h1_hi[:, :].bitcast(f32),
                                        ALU.subtract).then_inc(h1_lo_done, 1)

            def pair_coefficients(b, p):
                cols = slice(2 * p, 2 * p + 2)
                base = COEF_STEPS * b + PAIR_STEPS * p
                t0, t1, t2, t3, m = (ct[:, k, cols] for k in range(5))
                wait(pool, scored, T * b + 2 * p + 2)
                wait(pool, s_ready, b + 1)
                wait(pool, exps, T * (b - 1) + 2 * p + 2)
                wait(pool, coef_step, base)
                nc.gpsimd.tensor_tensor(t0, s_col[:, cols], dm[:, cols], ALU.add).then_inc(coef_step, 1)
                pool.wait_ge(coef_step, base + 1)
                nc.gpsimd.tensor_tensor(t2, t0, slopes[:, cols], ALU.mult).then_inc(coef_step, 1)
                nc.gpsimd.tensor_scalar(t1, t0, 0.0, 1.0 - SLOPE, ALU.max, ALU.mult).then_inc(coef_step, 1)
                pool.wait_ge(coef_step, base + 3)
                nc.gpsimd.tensor_tensor(m, t1, t2, ALU.add).then_inc(coef_step, 1)
                nc.gpsimd.tensor_tensor(t3, s_col[:, cols], slopes[:, cols], ALU.mult).then_inc(coef_step, 1)
                pool.wait_ge(coef_step, base + 5)
                nc.gpsimd.tensor_tensor(b1[:, cols], s_col[:, cols], m, ALU.subtract).then_inc(coef_step, 1)
                nc.gpsimd.tensor_tensor(b2[:, cols], t3, m, ALU.subtract).then_inc(coef_step, 1)

            def u2_low(b):
                wait(pool, u2_hi, b + 1)
                nc.gpsimd.tensor_tensor(u_lo[:, :], hn[:, :, :].rearrange("p k c -> p (k c)"),
                                        u_hi[:, :].bitcast(f32), ALU.subtract).then_inc(u2_lo, 1)

            def bias_xb(b):
                wait(pool, hw_read, b + 1)
                wait(pool, h_ready[2], b + 1)
                wait(pool, xb_biased, 2 * b)
                nc.gpsimd.tensor_tensor(c_row[:, :], hw_row[:, 1, :], bias2_row[:, :],
                                        ALU.add).then_inc(xb_biased, 1)
                pool.wait_ge(xb_biased, 2 * b + 1)
                nc.gpsimd.tensor_tensor(xb[:, :, :], xb[:, :, :],
                                        c_row[:, :].unsqueeze(1).broadcast_to([P, T, C]),
                                        ALU.add).then_inc(xb_biased, 1)

            def iteration(t):
                if exists(t):
                    h1_low(t)
                    pair_coefficients(t, 2)
                if exists(t + 2):
                    g_low(t + 2)
                    bias_xc(t + 2)
                if exists(t - 1):
                    coefficients(2, t - 1)
                if exists(t):
                    pair_coefficients(t, 3)
                if exists(t - 1):
                    u2_low(t - 1)
                if exists(t + 1):
                    pair_coefficients(t + 1, 0)
                if exists(t + 2):
                    coefficients(1, t + 2)
                if exists(t - 1):
                    bias_xb(t - 1)
                if exists(t + 3):
                    coefficients(0, t + 3)
                if exists(t + 1):
                    pair_coefficients(t + 1, 1)

            pool.wait_ge(w_ready, 1)
            coefficients(0, 0)
            g_low(0)
            bias_xc(0)
            coefficients(1, 0)
            coefficients(0, 1)
            g_low(1)
            bias_xc(1)
            pair_coefficients(0, 0)
            pair_coefficients(0, 1)
            coefficients(1, 1)
            coefficients(0, 2)
            for t in range(0, LOOP_FROM):
                iteration(t)
            with pool.Fori(LOOP_FROM, LOOP_TO) as t:
                iteration(t)
            for t in range(LOOP_TO, B + 1):
                iteration(t)

            for g in range(B // GROUP):
                for b in range(GROUP):
                    gb = g * GROUP + b
                    wait(pool, h3_ready, gb)
                    norm_coefficients(pool, st3, lt3, rstd3[:, :], nb3[:, :], stats3, gb + 1,
                                      ln3_step, gb * 10, None)

        @block.scalar
        def _(act):
            for dst, src in ((w_stage[:, 0, :], W0), (w_stage[:, 1, :], w1), (w2[:, :], W2),
                             (w_stage[:, 2, :], a_src.partition_broadcast(P)),
                             (w_stage[:, 3, :], a_dst.partition_broadcast(P)),
                             (b0_row[:, :], b0.partition_broadcast(P)),
                             (bias2_row[:, :], bias2.partition_broadcast(P)),
                             (gw_row[:, :], g_w.partition_broadcast(P)),
                             (gb_col[:, :], g_b.partition_broadcast(P))):
                act.dma_start(dst, src).then_inc(w_in, 16)

            for i in range(T):
                act.wait_ge(adj_in[i // 2], 16)
                if i >= 2:
                    act.wait_ge(rows_summed, i - 1)
                nc.scalar.activation(e2[:, i % 2, :], a_nat[:, i, :], ACT.Identity,
                                     accum_out=d_raw[:, i:i + 1]).then_inc(rows_summed, 1)
                act.wait_ge(at_tr, i + 1)
                nc.scalar.activation(at_hi[:, :, i * P:(i + 1) * P],
                                     tr[i % 2][:, :].rearrange("p (k i) -> p k i", i=P),
                                     ACT.Copy).then_inc(at_hi_done, 1)
            act.wait_ge(w0_tr, 1)
            nc.scalar.activation(w0t_hi[:, :], misc[:, 0:C], ACT.Copy).then_inc(w0_hi_done, 1)

            def apply_norm(L, b):
                wait(act, ln_step[L], LN_STEPS[L] * (b + 1))
                src, dst = [(xc, hn), (xa, xa), (xb, hn)][L]
                if L == 0:
                    wait(act, g_lo_done, b)
                    wait(act, u2_lo, b - 3)
                    wait(act, sji_step, 2 * T * (b - 3))
                if L == 1:
                    wait(act, x1_stored, 16 * (b + 1))
                if L == 2:
                    wait(act, g_lo_done, min(b + 4, B) if known(b) else b + 4)
                for k in range(T):
                    last = nc.scalar.activation(dst[:, k, :], src[:, k, :], ACT.Relu,
                                                bias=nb[L][:, k:k + 1], scale=rstd[L][:, k:k + 1])
                last.then_inc(h_ready[L], 1)

            def evacuate_hi(step, h, b, dst, done):
                k, n = side(f"{step}{h}", b)
                act.wait_ge(side_full[k], n + 1)
                nc.scalar.activation(dst[:, h * HALF:(h + 1) * HALF], side_bank[k][:, :],
                                     ACT.Copy).then_inc(done, 1)

            def stage_h1(b):
                wait(act, h1_lo_done, b)
                for h in range(2):
                    k, n = side(f"h1_{h}", b)
                    act.wait_ge(side_full[k], n + 1)
                    nc.scalar.activation(h1s[:, h * HALF:(h + 1) * HALF], side_bank[k][:, :],
                                         ACT.Copy).then_inc(side_free[k], 1)

            def split_h1(b):
                wait(act, pv_done, PAIRS * b)
                wait(act, *drained("h1_1", b))
                nc.scalar.activation(h1_hi[:, :], h1s[:, :], ACT.Copy).then_inc(h1_hi_done, 1)

            def spread_d(b):
                wait(act, scored, T * b)
                for h in range(2):
                    k, n = side(f"D{h}", b)
                    act.wait_ge(side_full[k], n + 1)
                    nc.scalar.activation(d_row[:, h * HALF:(h + 1) * HALF], side_bank[k][:, :],
                                         ACT.Copy).then_inc(side_free[k], 1)

            def exp_pair(b, p):
                wait(act, coef_step, COEF_STEPS * b + PAIR_STEPS * (p + 1))
                for a in range(2):
                    n, i = T * b + 2 * p + a, 2 * p + a
                    wait(act, p_max, n - 1)
                    nc.scalar.activation(e2[:, a, :], tm[:, i % 4, :], ACT.Exp,
                                         bias=b2[:, i:i + 1], scale=SLOPE).then_inc(e2_done, 1)
                    act.wait_ge(e2_done, n + 1)
                    nc.scalar.activation(tm[:, i % 4, :], tm[:, i % 4, :], ACT.Exp,
                                         bias=b1[:, i:i + 1]).then_inc(exps, 1)

            def pt_high(b, p):
                wait(act, pv_done, PAIRS * b + p - 1)
                for a in range(2):
                    act.wait_ge(p_tr, T * b + 2 * p + a + 1)
                    nc.scalar.activation(pt_hi[:, p % 2, :, a * P:(a + 1) * P],
                                         tr[a][:, :].rearrange("p (k i) -> p k i", i=P),
                                         ACT.Copy).then_inc(p_hi, 1)

            def evacuate_av(b, h):
                wait(act, pv_done, PAIRS * b + 2 * h + 2)
                nc.scalar.activation(avt[:, h * HALF:(h + 1) * HALF], pv_bank[:, :],
                                     ACT.Copy).then_inc(av_read, 1)

            def spread_hw(b):
                wait(act, hw_full, b + 1)
                wait(act, hw_added, b)
                nc.scalar.activation(hw_row[:, :, :].rearrange("p k c -> p (k c)"), misc[:, C:3 * C],
                                     ACT.Copy).then_inc(hw_read, 1)

            def iteration(t):
                if exists(t - 1):
                    pt_high(t - 1, 3)
                if exists(t + 1):
                    evacuate_hi("hT", 0, t + 1, u_hi, t_hi)
                    evacuate_hi("hT", 1, t + 1, u_hi, t_hi)
                if exists(t):
                    exp_pair(t, 1)
                    split_h1(t)
                if exists(t + 1):
                    stage_h1(t + 1)
                if exists(t - 1):
                    evacuate_av(t - 1, 1)
                if exists(t):
                    pt_high(t, 0)
                if exists(t + 2):
                    evacuate_hi("L0p", 0, t + 2, ot_hi, o0_hi)
                if exists(t):
                    exp_pair(t, 2)
                if exists(t + 2):
                    evacuate_hi("L0p", 1, t + 2, ot_hi, o0_hi)
                if exists(t):
                    pt_high(t, 1)
                if exists(t - 1):
                    apply_norm(2, t - 1)
                if exists(t + 1):
                    spread_d(t + 1)
                if exists(t):
                    exp_pair(t, 3)
                if exists(t):
                    evacuate_av(t, 0)
                    pt_high(t, 2)
                if exists(t - 1):
                    evacuate_hi("L2p", 0, t - 1, ot_hi, o2_hi)
                if exists(t + 2):
                    apply_norm(1, t + 2)
                if exists(t + 1):
                    exp_pair(t + 1, 0)
                if exists(t - 1):
                    evacuate_hi("L2p", 1, t - 1, ot_hi, o2_hi)
                    spread_hw(t - 1)
                if exists(t + 3):
                    apply_norm(0, t + 3)

            apply_norm(0, 0)
            evacuate_hi("L0p", 0, 0, ot_hi, o0_hi)
            evacuate_hi("L0p", 1, 0, ot_hi, o0_hi)
            apply_norm(1, 0)
            evacuate_hi("hT", 0, 0, u_hi, t_hi)
            evacuate_hi("hT", 1, 0, u_hi, t_hi)
            stage_h1(0)
            spread_d(0)
            apply_norm(0, 1)
            exp_pair(0, 0)
            evacuate_hi("L0p", 0, 1, ot_hi, o0_hi)
            evacuate_hi("L0p", 1, 1, ot_hi, o0_hi)
            apply_norm(1, 1)
            apply_norm(0, 2)
            for t in range(0, LOOP_FROM):
                iteration(t)
            with act.Fori(LOOP_FROM, LOOP_TO) as t:
                iteration(t)
            for t in range(LOOP_TO, B + 1):
                iteration(t)

            act.wait_ge(x3_stored, 16 * B)
            for g in range(B // GROUP):
                for b in range(GROUP):
                    gb = g * GROUP + b
                    wait(act, ln3_step, (gb + 1) * 10)
                    wait(act, ht_full, 2 * gb)
                    for k in range(T):
                        last = nc.scalar.activation(h3[:, k, :], xg[:, b, k, :], ACT.Relu,
                                                    bias=nb3[:, k:k + 1], scale=rstd3[:, k:k + 1])
                    last.then_inc(h3_ready, 1)
                    for h in range(2):
                        wait(act, ht_full, 2 * gb + h + 1)
                        wait(act, ring_full, g * RING_STEPS + b * T)
                        nc.scalar.activation(ht_hi[:, h * HALF:(h + 1) * HALF], side_bank[h][:, :],
                                             ACT.Copy).then_inc(ht_hi_done, 1)
                    for i in range(T):
                        n = b * T + i
                        wait(act, ring_full, g * RING_STEPS + n + 1)
                        nc.scalar.activation(uu_hi[0][:, i, b * C:(b + 1) * C], ring[n % 4][:, 0:C],
                                             ACT.Copy).then_inc(v_hi, 1)
                        nc.scalar.activation(v[0][:, i, b, :], ring[n % 4][:, C:2 * C], ACT.Copy)
                        nc.scalar.activation(v[1][:, i, b, :], ring[n % 4][:, 2 * C:3 * C],
                                             ACT.Copy).then_inc(v_copied, 1)
                for s in range(STAGES - 1):
                    for i in range(T):
                        wait(act, stage_sum, g * S_STEPS + s * T + i + 1)
                        nc.scalar.activation(uu_hi[(s + 1) % 2][:, i, :],
                                             v[s][:, i, :, :].rearrange("p b c -> p (b c)"),
                                             ACT.Copy).then_inc(stage_hi, 1)

        @block.vector
        def _(dve):
            dve.wait_ge(w_in, 9 * 16)
            dve.wait_ge(ident_done, 2)
            steps = [0]

            def w_step(ins):
                steps[0] += 1
                ins.then_inc(w_ready_dve, 1)

            w_step(nc.vector.tensor_copy(ident_r[:, :], ident[:, :]))
            w_step(nc.vector.tensor_copy(w1_hi[:, :], w_stage[:, 1, :]))
            w_step(nc.vector.tensor_tensor_reduce(junk[:, 0, :], w_stage[:, 1, :], w_stage[:, 2, :], 1.0, 0.0,
                                                  ALU.mult, ALU.add, wa_stage[:, 0:1]))
            w_step(nc.vector.tensor_tensor_reduce(junk[:, 1, :], w_stage[:, 1, :], w_stage[:, 3, :], 1.0, 0.0,
                                                  ALU.mult, ALU.add, wa_stage[:, 1:2]))
            w_step(nc.vector.tensor_scalar(w_stage[:, 4, :], w2[:, :], gw_row[:, 2 * C:2 * C + 1], None, ALU.mult))
            w_step(nc.vector.memset(sv_a[:, :, :].bitcast(f32), 1.0))
            w_step(nc.vector.memset(sv_b[:, :, :].bitcast(f32), 0.0))
            dve.wait_ge(w_ready_dve, 2)
            w_step(nc.vector.tensor_tensor(w1_lo[:, :], w_stage[:, 1, :], w1_hi[:, :].bitcast(f32), ALU.subtract))
            dve.wait_ge(w_ready_dve, 5)
            w_step(nc.vector.tensor_copy(wa_hi[:, :], wa_stage))
            w_step(nc.vector.tensor_copy(w2r_hi[:, :], w_stage[:, 4, :]))
            dve.wait_ge(w_ready_dve, 10)
            w_step(nc.vector.tensor_tensor(wa_lo[:, :], wa_stage, wa_hi[:, :].bitcast(f32), ALU.subtract))
            w_step(nc.vector.tensor_tensor(w2r_lo[:, :], w_stage[:, 4, :], w2r_hi[:, :].bitcast(f32), ALU.subtract))

            def norm_stats(L, b):
                if L == 0:
                    wait(dve, x_in, 16 * (b + 1))
                elif L == 1:
                    wait(dve, *drained("L0w1", b))
                else:
                    wait(dve, *drained("BT1", b))
                wait(dve, ln_step[L], LN_STEPS[L] * b)
                src = [xc, xa, xb][L]
                for k in range(T):
                    last = nc.vector.bn_stats(st[L][:, k, :], src[:, k, :])
                last.then_inc(stats[L], 1)

            norm_stats(0, 0)
            for i in range(T):
                dve.wait_ge(adj_in[i // 2], 16)
                nc.vector.tensor_scalar(mask[:, i, :], a_nat[:, i, :], 0.0, MASKED, ALU.is_le,
                                        ALU.mult).then_inc(mask_done, 1)
                dve.wait_ge(at_hi_done, i + 1)
                nc.vector.tensor_tensor(at_lo[:, :, i * P:(i + 1) * P],
                                        tr[i % 2][:, :].rearrange("p (k i) -> p k i", i=P),
                                        at_hi[:, :, i * P:(i + 1) * P].bitcast(f32),
                                        ALU.subtract).then_inc(at_lo_done, 1)
            dve.wait_ge(w_ready_dve, steps[0])
            dve.wait_ge(w0_hi_done, 1)
            nc.vector.tensor_tensor(w0t_lo[:, :], misc[:, 0:C], w0t_hi[:, :].bitcast(f32),
                                    ALU.subtract).then_inc(w_ready, 1)

            def split_g(b):
                wait(dve, h_ready[0], b + 1)
                if exists(b - 1):
                    wait(dve, *filled("L0p1", b - 1))
                nc.vector.tensor_copy(g_hi[:, :, :], hn[:, :, :]).then_inc(g_hi_done, 1)

            def evacuate_lo(step, h, b, hi, lo, hi_done):
                k, n = side(f"{step}{h}", b)
                dve.wait_ge(hi_done, 2 * b + h + 1)
                cols = slice(h * HALF, (h + 1) * HALF)
                nc.vector.tensor_tensor(lo[:, cols], side_bank[k][:, :], hi[:, cols].bitcast(f32),
                                        ALU.subtract).then_inc(side_free[k], 1)

            def residual0(b, h):
                k, n = side(f"L0w{h}", b)
                dve.wait_ge(side_full[k], n + 1)
                wait(dve, xc_biased, b + 1)
                if exists(b - 1):
                    wait(dve, *filled("hT1", b - 1))
                for q in range(HT):
                    i = h * HT + q
                    last = nc.vector.scalar_tensor_tensor(out=xa[:, i, :], in0=side_bank[k][:, q * P:(q + 1) * P],
                                                          scalar=d_col[:, i:i + 1], in1=xc[:, i, :],
                                                          op0=ALU.mult, op1=ALU.add)
                last.then_inc(side_free[k], 1)

            def score_pair(b, p):
                for a in range(2):
                    n, i = T * b + 2 * p + a, 2 * p + a
                    wait(dve, *drained("D1", b))
                    wait(dve, p_tr, n - 3)
                    nc.vector.memset(wait_cell[:, i % 4:i % 4 + 1], 0.0)
                    nc.vector.tensor_tensor_reduce(tm[:, i % 4, :], mask[:, i, :], d_row[:, :], 1.0, -3.4e38,
                                                   ALU.add, ALU.max, dm[:, i:i + 1]).then_inc(scored, 1)

            def max_pair(b, p):
                if p == 0:
                    wait(dve, rinv_done, b)
                for a in range(2):
                    n, i = T * b + 2 * p + a, 2 * p + a
                    dve.wait_ge(exps, n + 1)
                    nc.vector.scalar_tensor_tensor(out=tm[:, i % 4, :], in0=tm[:, i % 4, :], scalar=1.0,
                                                   in1=e2[:, a, :], op0=ALU.mult, op1=ALU.max,
                                                   accum_out=rsum[:, i:i + 1]).then_inc(p_max, 1)

            def pt_low(b, p):
                for a in range(2):
                    dve.wait_ge(p_hi, T * b + 2 * p + a + 1)
                    cols = slice(a * P, (a + 1) * P)
                    nc.vector.tensor_tensor(pt_lo[:, p % 2, :, cols],
                                            tr[a][:, :].rearrange("p (k i) -> p k i", i=P),
                                            pt_hi[:, p % 2, :, cols].bitcast(f32),
                                            ALU.subtract).then_inc(p_lo, 1)

            def copy_s(b):
                wait(dve, s_full, b + 1)
                wait(dve, coef_step, COEF_STEPS * b)
                nc.vector.tensor_copy(s_col[:, :], misc[:, 0:2 * T].rearrange("p (k w) -> p k w", w=2)[:, :, 0]
                                      ).then_inc(s_ready, 1)

            def invert_sums(b):
                wait(dve, p_max, T * (b + 1))
                if exists(b - 1):
                    wait(dve, *drained("BT1", b - 1))
                nc.vector.reciprocal(rinv[:, :], rsum[:, :]).then_inc(rinv_done, 1)

            def residual1(b, h):
                k, n = side(f"BT{h}", b)
                dve.wait_ge(side_full[k], n + 1)
                wait(dve, x1_loaded, 16 * (b + 1))
                wait(dve, rinv_done, b + 1)
                for q in range(HT):
                    i = h * HT + q
                    last = nc.vector.scalar_tensor_tensor(out=xb[:, i, :], in0=side_bank[k][:, q * P:(q + 1) * P],
                                                          scalar=rinv[:, i:i + 1], in1=xb[:, i, :],
                                                          op0=ALU.mult, op1=ALU.add)
                last.then_inc(side_free[k], 1)

            def split_u2(b):
                wait(dve, h_ready[2], b + 1)
                wait(dve, *filled("D1", min(b + 2, B - 1) if known(b) else b + 2))
                nc.vector.tensor_copy(u_hi[:, :], hn[:, :, :].rearrange("p k c -> p (k c)")).then_inc(u2_hi, 1)

            def node_scores(b):
                wait(dve, moments_done, b)
                wait(dve, hw_added, b)
                for w in range(2):
                    for k in range(T):
                        n = 2 * T * b + w * T + k
                        wait(dve, sji_step, n - 1 if w * T + k >= 2 else 2 * T * b)
                        nc.vector.tensor_tensor_reduce(junk[:, k % 2, :], hn[:, k, :], gw_row[:, w * C:(w + 1) * C],
                                                       1.0, 0.0, ALU.mult, ALU.add,
                                                       sji[:, w, k:k + 1]).then_inc(sji_step, 1)
                dve.wait_ge(sji_step, 2 * T * b + T)
                nc.vector.tensor_copy(sv_a[:, :, 1], sji[:, 0, :]).then_inc(sv_done, 1)
                dve.wait_ge(sv_done, 2 * b + 1)
                nc.vector.tensor_tensor(sv_b[:, :, 1], sji[:, 0, :], sv_a[:, :, 1].bitcast(f32),
                                        ALU.subtract).then_inc(sv_done, 1)

            def combine_moments(b):
                wait(dve, moments_done, b + 1)
                wait(dve, hw_full, b)
                nc.vector.tensor_copy(hg[:, 0:2], misc[:, 0:2]).then_inc(hg_step, 1)
                dve.wait_ge(hg_step, 2 * b + 1)
                nc.vector.scalar_tensor_tensor(out=hg[:, 2:3], in0=hg[:, 0:1], scalar=gb_col[:, 0:1],
                                               in1=hg[:, 1:2], op0=ALU.mult, op1=ALU.add).then_inc(hg_step, 1)

            def add_hw(b):
                wait(dve, xb_biased, 2 * b + 2)
                for k in range(T):
                    last = nc.vector.scalar_tensor_tensor(out=xb[:, k, :], in0=hw_row[:, 0, :],
                                                          scalar=sji[:, 1, k:k + 1], in1=xb[:, k, :],
                                                          op0=ALU.mult, op1=ALU.add)
                last.then_inc(hw_added, 1)

            def residual2(b, h):
                k, n = side(f"L2w{h}", b)
                dve.wait_ge(side_full[k], n + 1)
                wait(dve, hw_added, b + 1)
                rows = xb[:, h * HT:(h + 1) * HT, :].rearrange("p k c -> p (k c)")
                nc.vector.tensor_tensor(rows, side_bank[k][:, :], rows, ALU.add).then_inc(side_free[k], 1)

            def iteration(t):
                if exists(t):
                    max_pair(t, 0)
                if exists(t - 1):
                    pt_low(t - 1, 3)
                if exists(t + 1):
                    evacuate_lo("hT", 0, t + 1, u_hi, u_lo, t_hi)
                    evacuate_lo("hT", 1, t + 1, u_hi, u_lo, t_hi)
                if exists(t):
                    score_pair(t, 2)
                    max_pair(t, 1)
                    pt_low(t, 0)
                if exists(t - 1):
                    residual1(t - 1, 0)
                if exists(t + 2):
                    evacuate_lo("L0p", 0, t + 2, ot_hi, ot_lo, o0_hi)
                if exists(t - 1):
                    residual1(t - 1, 1)
                    norm_stats(2, t - 1)
                if exists(t):
                    score_pair(t, 3)
                    max_pair(t, 2)
                    pt_low(t, 1)
                if exists(t + 2):
                    evacuate_lo("L0p", 1, t + 2, ot_hi, ot_lo, o0_hi)
                if exists(t + 1):
                    copy_s(t + 1)
                if exists(t - 1):
                    split_u2(t - 1)
                    node_scores(t - 1)
                if exists(t + 2):
                    residual0(t + 2, 0)
                    residual0(t + 2, 1)
                if exists(t + 1):
                    score_pair(t + 1, 0)
                if exists(t):
                    max_pair(t, 3)
                    pt_low(t, 2)
                    invert_sums(t)
                if exists(t + 2):
                    norm_stats(1, t + 2)
                if exists(t - 1):
                    combine_moments(t - 1)
                    evacuate_lo("L2p", 0, t - 1, ot_hi, ot_lo, o2_hi)
                if exists(t + 1):
                    score_pair(t + 1, 1)
                if exists(t - 1):
                    evacuate_lo("L2p", 1, t - 1, ot_hi, ot_lo, o2_hi)
                if exists(t + 3):
                    norm_stats(0, t + 3)
                if exists(t - 1):
                    add_hw(t - 1)
                    residual2(t - 1, 0)
                    residual2(t - 1, 1)
                if exists(t + 3):
                    split_g(t + 3)

            split_g(0)
            evacuate_lo("L0p", 0, 0, ot_hi, ot_lo, o0_hi)
            evacuate_lo("L0p", 1, 0, ot_hi, ot_lo, o0_hi)
            residual0(0, 0)
            residual0(0, 1)
            norm_stats(1, 0)
            norm_stats(0, 1)
            evacuate_lo("hT", 0, 0, u_hi, u_lo, t_hi)
            evacuate_lo("hT", 1, 0, u_hi, u_lo, t_hi)
            copy_s(0)
            score_pair(0, 0)
            score_pair(0, 1)
            split_g(1)
            evacuate_lo("L0p", 0, 1, ot_hi, ot_lo, o0_hi)
            evacuate_lo("L0p", 1, 1, ot_hi, ot_lo, o0_hi)
            residual0(1, 0)
            residual0(1, 1)
            norm_stats(1, 1)
            norm_stats(0, 2)
            split_g(2)
            for t in range(0, LOOP_FROM):
                iteration(t)
            with dve.Fori(LOOP_FROM, LOOP_TO) as t:
                iteration(t)
            for t in range(LOOP_TO, B + 1):
                iteration(t)

            dve.wait_ge(w3_in, 16)
            for k in range(STAGES):
                nc.vector.tensor_tensor(w3_sum[:, k, :], w3_raw[:, :, STAGES - k], w3_raw[:, :, 2 * STAGES - k],
                                        ALU.add).then_inc(w3_step, 1)
            nc.vector.tensor_copy(w3_sum[:, STAGES, :], w3_raw[:, :, 0]).then_inc(w3_step, 1)
            dve.wait_ge(w3_step, 4)
            w3_flat = w3_sum[:, :, :].rearrange("p k c -> p (k c)")
            nc.vector.tensor_copy(w3_hi[:, :], w3_flat).then_inc(w3_step, 1)
            dve.wait_ge(w3_step, 5)
            nc.vector.tensor_tensor(w3_lo[:, :], w3_flat, w3_hi[:, :].bitcast(f32), ALU.subtract).then_inc(w3_step, 1)
            dve.wait_ge(w3_step, 6)
            nc.vector.memset(lt3[:, 7, 0:1], 0.0).then_inc(ring_free, 4)

            def stats_of(g, b):
                gb = g * GROUP + b
                dve.wait_ge(xg_in[b], g * 16 + 16)
                dve.wait_ge(ln3_step, gb * 10)
                for k in range(T):
                    last = nc.vector.bn_stats(st3[:, k, :], xg[:, b, k, :])
                last.then_inc(stats3, 1)

            for g in range(B // GROUP):
                stats_of(g, 0)
                for b in range(GROUP):
                    gb = g * GROUP + b
                    for h in range(2):
                        cols = slice(h * HALF, (h + 1) * HALF)
                        wait(dve, ht_hi_done, 2 * gb + h + 1)
                        nc.vector.tensor_tensor(ht_lo[:, cols], side_bank[h][:, :], ht_hi[:, cols].bitcast(f32),
                                                ALU.subtract).then_inc(ht_lo_done, 1)
                    if b + 1 < GROUP:
                        stats_of(g, b + 1)
                    for i in range(T):
                        n = b * T + i
                        wait(dve, v_copied, g * V_STEPS + n + 1)
                        nc.vector.tensor_tensor(uu_lo[0][:, i, b * C:(b + 1) * C], ring[n % 4][:, 0:C],
                                                uu_hi[0][:, i, b * C:(b + 1) * C].bitcast(f32),
                                                ALU.subtract).then_inc(v_read, 1)
                        wait(dve, h3_ready, gb + 1)
                        nc.vector.tensor_tensor(xg[:, b, i, :], ring[n % 4][:, 3 * C:4 * C], xg[:, b, i, :],
                                                ALU.add).then_inc(ring_free, 1)
                for s in range(STAGES):
                    for i in range(T):
                        n = V_STEPS + s * T + i
                        wait(dve, ring_full, g * RING_STEPS + n + 1)
                        if s < STAGES - 1:
                            nc.vector.tensor_tensor(v[s][:, i, :, :].rearrange("p b c -> p (b c)"), ring[n % 4][:, :],
                                                    v[s][:, i, :, :].rearrange("p b c -> p (b c)"),
                                                    ALU.add).then_inc(stage_sum, 1)
                            wait(dve, stage_hi, g * (2 * T) + s * T + i + 1)
                            nc.vector.tensor_tensor(uu_lo[(s + 1) % 2][:, i, :],
                                                    v[s][:, i, :, :].rearrange("p b c -> p (b c)"),
                                                    uu_hi[(s + 1) % 2][:, i, :].bitcast(f32),
                                                    ALU.subtract).then_inc(stage_lo, 1)
                            wait(dve, stage_lo, g * (2 * T) + s * T + i + 1)
                            nc.vector.memset(lt3[:, 7, 0:1], 0.0).then_inc(ring_free, 1)
                        else:
                            nc.vector.tensor_tensor(xg[:, :, i, :],
                                                    ring[n % 4][:, :].rearrange("p (b c) -> p b c", c=C),
                                                    xg[:, :, i, :], ALU.add).then_inc(stage_sum, 1)
                            wait(dve, stage_sum, g * S_STEPS + s * T + i + 1)
                            nc.vector.memset(lt3[:, 7, 0:1], 0.0).then_inc(ring_free, 1)

        @block.tensor
        def _(pe):
            def turn(dst, src):
                return nc.tensor.transpose(dst, src, ident[:, :])

            pe.wait_ge(ident_done, 2)
            for i in range(T):
                pe.wait_ge(adj_in[i // 2], 16)
                if i >= 2:
                    pe.wait_ge(at_lo_done, i - 1)
                for j in range(T):
                    last = turn(tr[i % 2][:, j * P:(j + 1) * P], a_nat[:, i, j * P:(j + 1) * P])
                last.then_inc(at_tr, 1)
            pe.wait_ge(w_in, 9 * 16)
            turn(misc[:, 0:C], w_stage[:, 0, :]).then_inc(w0_tr, 1)
            pe.wait_ge(w_ready, 1)
            pe.wait_ge(at_lo_done, T)

            def take(step, b):
                k, n = side(step, b)
                wait(pe, side_free[k], n)
                return side_bank[k], side_full[k]

            def propagate(bank, hi, lo, h, plus_identity):
                cols = slice(h * HALF, (h + 1) * HALF)
                for j in range(T):
                    nc.tensor.matmul(bank[:, :], hi(j), at_lo[:, j, cols], start=(j == 0), stop=False,
                                     skip_group_check=True)
                    if plus_identity and j // HT == h:
                        own = bank[:, (j % HT) * P:(j % HT + 1) * P]
                        for w in (hi, lo):
                            nc.tensor.matmul(own, w(j), ident_r[:, :], start=False, stop=False,
                                             skip_group_check=True)
                    nc.tensor.matmul(bank[:, :], hi(j), at_hi[:, j, cols], start=False, stop=False,
                                     skip_group_check=True)
                    last = nc.tensor.matmul(bank[:, :], lo(j), at_hi[:, j, cols], start=False,
                                            stop=(j == T - 1), skip_group_check=True)
                return last

            def tiles_of(tensor):
                return lambda j: tensor[:, j, :]

            def blocks_of(tensor):
                return lambda j: tensor[:, j * P:(j + 1) * P]

            def product(dst, l_hi, l_lo, r_hi, r_lo):
                nc.tensor.matmul(dst, l_hi, r_lo, start=True, stop=False)
                nc.tensor.matmul(dst, l_hi, r_hi, start=False, stop=False)
                return nc.tensor.matmul(dst, l_lo, r_hi, start=False, stop=True)

            def l0_propagate(b, h):
                wait(pe, g_lo_done, b + 1)
                bank, full = take(f"L0p{h}", b)
                propagate(bank, tiles_of(g_hi), tiles_of(g_lo), h, True).then_inc(full, 1)

            def rows_out(step, prop, b, h, r_hi, r_lo):
                wait(pe, *drained(f"{prop}{h}", b))
                bank, full = take(f"{step}{h}", b)
                for q in range(HT):
                    block_ = slice((h * HT + q) * P, (h * HT + q + 1) * P)
                    last = product(bank[:, q * P:(q + 1) * P], ot_hi[:, block_], ot_lo[:, block_], r_hi, r_lo)
                last.then_inc(full, 1)

            def l1_turn(b):
                wait(pe, h_ready[1], b + 1)
                for h in range(2):
                    bank, full = take(f"hT{h}", b)
                    for q in range(HT):
                        last = turn(bank[:, q * P:(q + 1) * P], xa[:, h * HT + q, :])
                    last.then_inc(full, 1)

            def l1_project(b):
                wait(pe, hw_read, b - 2)
                for h in range(2):
                    wait(pe, *drained(f"hT{h}", b))
                    bank, full = take(f"h1_{h}", b)
                    for q in range(HT):
                        i = h * HT + q
                        hi, lo = u_hi[:, i * P:(i + 1) * P], u_lo[:, i * P:(i + 1) * P]
                        last = product(bank[:, q * P:(q + 1) * P], hi, lo, w1_hi[:, :], w1_lo[:, :])
                        tiny = product(misc[:, 2 * i:2 * i + 2], hi, lo, wa_hi[:, :], wa_lo[:, :])
                    last.then_inc(full, 1)
                tiny.then_inc(s_full, 1)

            def l1_rows(b):
                for h in range(2):
                    cols = slice(h * HALF, (h + 1) * HALF)
                    bank, full = take(f"D{h}", b)
                    product(bank[:, :], wa_hi[:, 1:2].broadcast_to([P, P]), wa_lo[:, 1:2].broadcast_to([P, P]),
                            u_hi[:, cols], u_lo[:, cols]).then_inc(full, 1)

            def turn_p(b, p):
                for a in range(2):
                    n, i = T * b + 2 * p + a, 2 * p + a
                    pe.wait_ge(p_max, n + 1)
                    wait(pe, p_lo, n - 1)
                    for j in range(T):
                        last = turn(tr[a][:, j * P:(j + 1) * P], tm[:, i % 4, j * P:(j + 1) * P])
                    last.then_inc(p_tr, 1)

            def attend(b, p):
                wait(pe, p_lo, T * b + 2 * p + 2)
                wait(pe, h1_lo_done, b + 1)
                wait(pe, av_read, 2 * b + p // 2)
                dst = pv_bank[:, (p % 2) * 2 * P:(p % 2 + 1) * 2 * P]
                for j in range(T):
                    block_ = slice(j * P, (j + 1) * P)
                    for w, m in ((h1_hi, pt_lo), (h1_hi, pt_hi), (h1_lo, pt_hi)):
                        last = nc.tensor.matmul(dst, w[:, block_], m[:, p % 2, j, :],
                                                start=(j == 0 and w is h1_hi and m is pt_lo),
                                                stop=(j == T - 1 and w is h1_lo))
                last.then_inc(pv_done, 1)

            def turn_back(b, h):
                wait(pe, av_read, 2 * b + h + 1)
                bank, full = take(f"BT{h}", b)
                for q in range(HT):
                    i = h * HT + q
                    last = turn(bank[:, q * P:(q + 1) * P], avt[:, i * P:(i + 1) * P])
                last.then_inc(full, 1)

            def l2_moments(b):
                wait(pe, u2_lo, b + 1)
                wait(pe, sv_done, 2 * b + 2)
                wait(pe, s_ready, min(b + 3, B) if known(b) else b + 3)
                for j in range(T):
                    block_ = slice(j * P, (j + 1) * P)
                    for w, m in ((u_hi, sv_b), (u_hi, sv_a), (u_lo, sv_a)):
                        last = nc.tensor.matmul(misc[:, 0:2], w[:, block_], m[:, j, :],
                                                start=(j == 0 and w is u_hi and m is sv_b),
                                                stop=(j == T - 1 and w is u_lo))
                last.then_inc(moments_done, 1)

            def l2_propagate(b, h):
                bank, full = take(f"L2p{h}", b)
                propagate(bank, blocks_of(u_hi), blocks_of(u_lo), h, False).then_inc(full, 1)

            def l2_rows(b):
                wait(pe, hg_step, 2 * b + 2)
                nc.tensor.matmul(misc[:, C:2 * C], hg[:, 0:1].broadcast_to([P, P]), w2[:, :], start=True, stop=True)
                nc.tensor.matmul(misc[:, 2 * C:3 * C], hg[:, 2:3].broadcast_to([P, P]), w2[:, :],
                                 start=True, stop=True).then_inc(hw_full, 1)

            def iteration(t):
                if exists(t + 1):
                    l1_turn(t + 1)
                if exists(t):
                    turn_p(t, 0)
                if exists(t - 1):
                    attend(t - 1, 3)
                if exists(t + 1):
                    l1_project(t + 1)
                if exists(t + 2):
                    l0_propagate(t + 2, 0)
                if exists(t):
                    turn_p(t, 1)
                if exists(t - 1):
                    turn_back(t - 1, 0)
                    turn_back(t - 1, 1)
                if exists(t):
                    attend(t, 0)
                if exists(t + 2):
                    l0_propagate(t + 2, 1)
                if exists(t + 1):
                    l1_rows(t + 1)
                if exists(t):
                    turn_p(t, 2)
                    attend(t, 1)
                if exists(t + 2):
                    rows_out("L0w", "L0p", t + 2, 0, w0t_hi[:, :], w0t_lo[:, :])
                    rows_out("L0w", "L0p", t + 2, 1, w0t_hi[:, :], w0t_lo[:, :])
                if exists(t - 1):
                    l2_moments(t - 1)
                    l2_propagate(t - 1, 0)
                if exists(t):
                    turn_p(t, 3)
                    attend(t, 2)
                if exists(t - 1):
                    l2_propagate(t - 1, 1)
                    l2_rows(t - 1)
                    rows_out("L2w", "L2p", t - 1, 0, w2r_hi[:, :], w2r_lo[:, :])
                    rows_out("L2w", "L2p", t - 1, 1, w2r_hi[:, :], w2r_lo[:, :])

            l0_propagate(0, 0)
            l0_propagate(0, 1)
            rows_out("L0w", "L0p", 0, 0, w0t_hi[:, :], w0t_lo[:, :])
            rows_out("L0w", "L0p", 0, 1, w0t_hi[:, :], w0t_lo[:, :])
            l1_turn(0)
            l1_project(0)
            l1_rows(0)
            l0_propagate(1, 0)
            l0_propagate(1, 1)
            rows_out("L0w", "L0p", 1, 0, w0t_hi[:, :], w0t_lo[:, :])
            rows_out("L0w", "L0p", 1, 1, w0t_hi[:, :], w0t_lo[:, :])
            for t in range(0, LOOP_FROM):
                iteration(t)
            with pe.Fori(LOOP_FROM, LOOP_TO) as t:
                iteration(t)
            for t in range(LOOP_TO, B + 1):
                iteration(t)

            pe.wait_ge(w3_step, 6)
            for g in range(B // GROUP):
                for b in range(GROUP):
                    gb = g * GROUP + b
                    wait(pe, h3_ready, gb + 1)
                    wait(pe, ht_lo_done, 2 * gb)
                    for h in range(2):
                        for q in range(HT):
                            last = turn(side_bank[h][:, q * P:(q + 1) * P], h3[:, h * HT + q, :])
                        last.then_inc(ht_full, 1)
                    for i in range(T):
                        n = b * T + i
                        wait(pe, ht_lo_done, 2 * gb + i // HT + 1)
                        wait(pe, ring_free, g * RING_STEPS + n + 1)
                        product(ring[n % 4][:, :], ht_hi[:, i * P:(i + 1) * P], ht_lo[:, i * P:(i + 1) * P],
                                w3_hi[:, :], w3_lo[:, :]).then_inc(ring_full, 1)
                for s in range(STAGES):
                    hi, lo = uu_hi[s % 2], uu_lo[s % 2]
                    for i in range(T):
                        n = V_STEPS + s * T + i
                        rows = slice(i * P, (i + 1) * P)
                        wait(pe, ring_free, g * RING_STEPS + n + 1)
                        for j in range(T):
                            if i == 0 and s == 0 and j == 0:
                                wait(pe, v_read, g * V_STEPS + V_STEPS)
                            if i == 0 and s > 0:
                                wait(pe, stage_lo, g * (2 * T) + (s - 1) * T + j + 1)
                            for w, m in ((at_lo, hi), (at_hi, hi), (at_hi, lo)):
                                last = nc.tensor.matmul(ring[n % 4][:, :], w[:, j, rows], m[:, j, :],
                                                        start=(j == 0 and w is at_lo),
                                                        stop=(j == T - 1 and m is lo))
                        last.then_inc(ring_full, 1)


_INS = ["x", "adj", "L0_gnn_W", "L0_gnn_b", "L1_gnn_w", "L1_gnn_a_src", "L1_gnn_a_dst", "L2_gnn_g_w",
        "L2_gnn_g_b", "L2_gnn_weight", "L2_gnn_bias", "L3_gnn_weight_1"]


def kernel(**inputs):
    import numpy as _np
    import concourse.bacc as _bacc
    from concourse import mybir as _mybir
    from concourse.bass_utils import run_bass_kernel_spmd as _run

    nc = _bacc.Bacc("TRN2", target_bir_lowering=False, num_devices=1)
    arrays, args = {}, []
    for name in _INS:
        a = _np.ascontiguousarray(inputs[name])
        if a.ndim == 0:
            a = a.reshape(1)
        arrays[f"in_{name}"] = a
        args.append(nc.dram_tensor(f"in_{name}", a.shape, _mybir.dt.from_np(a.dtype), kind="ExternalInput").ap())
    args.append(nc.dram_tensor("out_0", (B, N, C), _mybir.dt.float32, kind="ExternalOutput").ap())
    build(nc, *args)
    r = _run(nc, [arrays], core_ids=[0])
    return r.results[0]["out_0"]
```

```python
import concourse.bass as bass
from concourse import mybir
from contextlib import ExitStack

B, N, C = 8, 1024, 128
P = 128
T = N // P
HALF = N // 2
HT = T // 2
PAIRS = T // 2
EPS = 1e-5
SLOPE = 0.2
MASKED = -3.0e38
KDIM = 7
GROUP = 4
STAGES = 3

SIDE_STEPS = [("BT0", -1, 1), ("L0p0", 2, 0), ("L0p1", 2, 1), ("BT1", -1, 0), ("L0w0", 2, 0), ("L0w1", 2, 1),
              ("h1_0", 1, 0), ("h1_1", 1, 1), ("D0", 1, 0), ("D1", 1, 0), ("h1_2", 1, 1), ("L2p0", -1, 1),
              ("L2p1", -1, 0), ("L2w0", -1, 1), ("L2w1", -1, 0), ("hT0", 2, 1), ("hT1", 2, 0)]
H1_TILES = (range(0, 3), range(3, 6), range(6, 8))
FIRST, LAST = -3, B + 1
LOOP_FROM, LOOP_TO = 2, B - 3


def ring_order():
    order = [("V", b, i) for b in range(GROUP) for i in range(T)]
    order += [("S", 0, s, i) for s in range(STAGES - 1) for i in range(T)]
    for k in range(GROUP):
        order.append(("S", 0, STAGES - 1, 2 * k))
        order += [("V", GROUP + k, i) for i in range(T)]
        order.append(("S", 0, STAGES - 1, 2 * k + 1))
    return order + [("S", 1, s, i) for s in range(STAGES) for i in range(T)]


RING = {content: n for n, content in enumerate(ring_order())}


def known(v):
    return isinstance(v, int)


def exists(b):
    return not known(b) or 0 <= b < B


def side_fills():
    fills, counts = {}, [0, 0]
    for t in range(FIRST, LAST):
        for step, offset, bank in SIDE_STEPS:
            if 0 <= t + offset < B:
                fills[step, t + offset] = bank, counts[bank]
                counts[bank] += 1
    return fills


SIDE_FILLS = side_fills()
SIDE_OFFSET = {step: offset for step, offset, _ in SIDE_STEPS}
FILLS_PER_ITERATION = [sum(bank == k for _, _, bank in SIDE_STEPS) for k in range(2)]


def side(step, b):
    if known(b):
        return SIDE_FILLS[step, b]
    first = SIDE_OFFSET[step] + LOOP_FROM
    bank, n = SIDE_FILLS[step, first]
    assert all(SIDE_FILLS[step, first + k] == (bank, n + k * FILLS_PER_ITERATION[bank])
               for k in range(LOOP_TO - LOOP_FROM))
    return bank, (b - first) * FILLS_PER_ITERATION[bank] + n


def for_batches(step):
    def guarded(*args):
        if exists(args[0]):
            step(*args)
    return guarded


def wait(eng, sem, value):
    if not known(value) or value > 0:
        eng.wait_ge(sem, value)


def build(nc, x, adj, W0, b0, w1, a_src, a_dst, g_w, g_b, W2, bias2, W3, out):
    f32, f32r, bf16 = mybir.dt.float32, mybir.dt.float32r, mybir.dt.bfloat16
    ALU, ACT = mybir.AluOpType, mybir.ActivationFunctionType
    ctx = ExitStack()
    with ctx:
        x1_dram = nc.dram_tensor("x1_scratch", (B, P, N), f32, kind="Internal").ap()
        x3_dram = nc.dram_tensor("x3_scratch", (B, P, N), f32, kind="Internal").ap()

        def sem(name):
            return ctx.enter_context(nc.semaphore(name))

        def keep(name, shape, dt=f32):
            return ctx.enter_context(nc.sbuf_tensor(name, shape, dt))

        at_hi = keep("at_hi", [P, T, N], f32r)
        at_lo = keep("at_lo", [P, T, N], f32r)
        ident = keep("ident", [P, P])
        neg_half = keep("neg_half", [P, T])
        st3 = keep("st3", [P, T, 6])
        lt3 = keep("lt3", [P, 7, T])
        rstd3 = keep("rstd3", [P, T])
        nb3 = keep("nb3", [P, T])

        phase1 = ExitStack()

        def sb(name, shape, dt=f32):
            return phase1.enter_context(nc.sbuf_tensor(name, shape, dt))

        xb = sb("xb", [P, T, C])
        hn = sb("hn", [P, T, C])
        u = sb("u", [P, 2, N], f32r)
        u_hi, u_lo = u[:, 0, :], u[:, 1, :]
        ot_hi = sb("ot_hi", [P, N], f32r)
        ot_lo = sb("ot_lo", [P, N], f32r)
        avt = sb("avt", [P, N])
        w2 = sb("w2", [P, C])
        w2r_hi = sb("w2r_hi", [P, C], f32r)
        w2r_lo = sb("w2r_lo", [P, C], f32r)
        bias2_row = sb("bias2_row", [P, C])
        gw_row = sb("gw_row", [P, 2 * C + 1])
        hw_row = sb("hw_row", [P, 2, C])
        c_row = sb("c_row", [P, C])
        junk = sb("junk", [P, 2, C], bf16)
        rsum = sb("rsum", [P, T])
        rinv = sb("rinv", [P, T])
        sji = sb("sji", [P, 2, T])
        sv = sb("sv", [P, T, 3], f32r)
        moments = sb("moments", [P, 2 * C])
        pick = sb("pick", [P, 2, 6])
        small = sb("small", [P, 16])
        hg = small[:, 0:2]
        wait_cell, junk_hg = small[:, 2:6], small[:, 6:12]
        gb_col = small[:, 12:13]
        st, lt, rstd, nb = [st3], [lt3], [rstd3], [nb3]
        for k in (2, 1):
            st.insert(1, sb(f"st{k}", [P, T, 6]))
            lt.insert(1, sb(f"lt{k}", [P, 7, T]))
            rstd.insert(1, sb(f"rstd{k}", [P, T]))
            nb.insert(1, sb(f"nb{k}", [P, T]))
        h1s = sb("h1s", [P, T, C + 2])
        xc = sb("xc", [P, T, C])
        g_hi = sb("g_hi", [P, T, C], f32r)
        g_lo = sb("g_lo", [P, T, C], f32r)
        xa = sb("xa", [P, T, C])
        mask = sb("mask", [P, T, N], bf16)
        d_row = sb("d_row", [P, N])
        h1_hi = sb("h1_hi", [P, N], f32r)
        h1_lo = sb("h1_lo", [P, N], f32r)
        e2 = sb("e2", [P, 2, N])
        tm = sb("tm", [P, 4, N])
        w0t_hi = sb("w0t_hi", [P, C], f32r)
        w0t_lo = sb("w0t_lo", [P, C], f32r)
        w1_hi = sb("w1_hi", [P, C + 2], f32r)
        w1_lo = sb("w1_lo", [P, C + 2], f32r)
        ident_r = sb("ident_r", [P, P], f32r)
        b0_row = sb("b0_row", [P, C])
        dm = sb("dm", [P, T])
        s_col = sb("s_col", [P, T])
        b1 = sb("b1", [P, T])
        b2 = sb("b2", [P, T])
        ct = sb("ct", [P, 5, T])
        slopes = sb("slopes", [P, T])
        d_raw = sb("d_raw", [P, T])
        d_col = sb("d_col", [P, T])
        with ExitStack() as setup:
            a_nat = setup.enter_context(nc.sbuf_tensor("a_nat", [P, T, N], f32))
        pt_hi = sb("pt_hi", [P, 2, T, 2 * P], f32r)
        pt_lo = sb("pt_lo", [P, 2, T, 2 * P], f32r)
        w_stage = tm[:, 0, :].rearrange("p (k c) -> p k c", c=C)
        w1a_stage = tm[:, 1, 0:C + 2]
        phase1.close()

        phase2 = ExitStack()

        def sb2(name, shape, dt=f32):
            return phase2.enter_context(nc.sbuf_tensor(name, shape, dt))

        uu_hi, uu_lo, xg = [None, None], [None, None], [None, None]
        uu_hi[1] = sb2("uu_hi1", [P, T, GROUP * C], f32r)
        uu_lo[1] = sb2("uu_lo1", [P, T, GROUP * C], f32r)
        xg[1] = sb2("xg1", [P, GROUP, T, C])
        w3_hi = sb2("w3_hi", [P, 4 * C], f32r)
        w3_lo = sb2("w3_lo", [P, 4 * C], f32r)
        xg[0] = sb2("xg0", [P, GROUP, T, C])
        ht_hi = sb2("ht_hi", [P, N], f32r)
        with ExitStack() as before_split:
            h3_late = before_split.enter_context(nc.sbuf_tensor("h3_late", [P, T, C], f32))
        ht_lo = sb2("ht_lo", [P, N], f32r)
        uu_hi[0] = sb2("uu_hi0", [P, T, GROUP * C], f32r)
        uu_lo[0] = sb2("uu_lo0", [P, T, GROUP * C], f32r)
        v = sb2("v", [P, 2, T, GROUP, C])
        phase2.close()
        w3_raw = xc[:, :, :].rearrange("p k c -> p (k c)")[:, 0:C * KDIM].rearrange("p (c k) -> p c k", k=KDIM)
        w3_sum = xa[:, 0:STAGES + 1, :]

        tr = [ctx.enter_context(nc.psum_tensor(f"tr{k}", [P, N], f32)) for k in range(2)]
        pv_bank = ctx.enter_context(nc.psum_tensor("pv_bank", [P, HALF], f32))
        misc = ctx.enter_context(nc.psum_tensor("misc", [P, HALF], f32))
        side_bank = [ctx.enter_context(nc.psum_tensor(f"side{k}", [P, HALF], f32)) for k in range(2)]
        ring = [tr[0][:, 0:HALF], tr[0][:, HALF:N], tr[1][:, 0:HALF], tr[1][:, HALF:N]]

        adj_in = [sem(f"adj_in{k}") for k in range(4)]
        w_in, x_in = sem("w_in"), sem("x_in")
        ident_done, mask_done, rows_summed = sem("ident_done"), sem("mask_done"), sem("rows_summed")
        at_tr, at_hi_done, at_lo_done = sem("at_tr"), sem("at_hi_done"), sem("at_lo_done")
        w0_tr, w0_hi_done = sem("w0_tr"), sem("w0_hi_done")
        w_ready, w_ready_dve, d_step = sem("w_ready"), sem("w_ready_dve"), sem("d_step")
        side_full = [sem(f"side_full{k}") for k in range(2)]
        side_free = [sem(f"side_free{k}") for k in range(2)]
        x1_stored, x1_loaded, x3_stored = sem("x1_stored"), sem("x1_loaded"), sem("x3_stored")
        stats = [sem(f"stats{k}") for k in range(3)]
        ln_step = [sem(f"ln_step{k}") for k in range(3)]
        h_ready = [sem(f"h_ready{k}") for k in range(3)]
        g_hi_done, g_lo_done, xc_biased = sem("g_hi_done"), sem("g_lo_done"), sem("xc_biased")
        o0_hi, o2_hi, t_hi = sem("o0_hi"), sem("o2_hi"), sem("t_hi")
        h1_hi_done, h1_lo_done = sem("h1_hi_done"), sem("h1_lo_done")
        s_ready = sem("s_ready")
        scored, coef_step, exps = sem("scored"), sem("coef_step"), sem("exps")
        e2_done = sem("e2_done")
        p_max, p_tr, p_hi, p_lo = sem("p_max"), sem("p_tr"), sem("p_hi"), sem("p_lo")
        pv_done, av_read, rinv_done = sem("pv_done"), sem("av_read"), sem("rinv_done")
        u2_hi, u2_lo = sem("u2_hi"), sem("u2_lo")
        sji_step, sv_done = sem("sji_step"), sem("sv_done")
        moments_read, moments_turned = sem("moments_read"), sem("moments_turned")
        moments_done, hg_step, hw_full, hw_read = sem("moments_done"), sem("hg_step"), sem("hw_full"), sem("hw_read")
        xb_biased, hw_added = sem("xb_biased"), sem("hw_added")

        def filled(step, b):
            k, n = side(step, b)
            return side_full[k], n + 1

        def drained(step, b):
            k, n = side(step, b)
            return side_free[k], n + 1

        LN_STEPS = [11, 10, 10]
        PAIR_STEPS = 7
        COEF_STEPS = PAIR_STEPS * PAIRS

        def norm_coefficients(eng, s, l, rs, n_b, stats_sem, have, step_sem, base, scale_col,
                              make_scale=None):
            wait(eng, stats_sem, have)
            wait(eng, step_sem, base)
            total, delta, square, var, part, sum_v, neg_mean = (l[:, k, :] for k in range(7))
            nc.gpsimd.tensor_tensor(total, s[:, :, 1], s[:, :, 4], ALU.add).then_inc(step_sem, 1)
            nc.gpsimd.tensor_tensor(delta, s[:, :, 1], s[:, :, 4], ALU.subtract).then_inc(step_sem, 1)
            nc.gpsimd.tensor_tensor(square, s[:, :, 2], s[:, :, 5], ALU.add).then_inc(step_sem, 1)
            eng.wait_ge(step_sem, base + 3)
            nc.gpsimd.tensor_tensor(part, delta, neg_half[:, :], ALU.mult).then_inc(step_sem, 1)
            nc.gpsimd.tensor_scalar(var, square, 1.0 / C, EPS, ALU.mult, ALU.add).then_inc(step_sem, 1)
            nc.gpsimd.tensor_tensor(neg_mean, total, neg_half[:, :], ALU.mult).then_inc(step_sem, 1)
            eng.wait_ge(step_sem, base + 4)
            nc.gpsimd.tensor_tensor(delta, part, part, ALU.mult).then_inc(step_sem, 1)
            eng.wait_ge(step_sem, base + 7)
            nc.gpsimd.tensor_tensor(sum_v, var, delta, ALU.add).then_inc(step_sem, 1)
            eng.wait_ge(step_sem, base + 8)
            if scale_col is None:
                nc.gpsimd.tensor_tensor(rs, sum_v, neg_half[:, :], ALU.pow).then_inc(step_sem, 1)
                eng.wait_ge(step_sem, base + 9)
            else:
                nc.gpsimd.tensor_tensor(part, sum_v, neg_half[:, :], ALU.pow).then_inc(step_sem, 1)
                eng.wait_ge(step_sem, base + 9)
                if make_scale:
                    make_scale()
                nc.gpsimd.tensor_tensor(rs, part, scale_col, ALU.mult).then_inc(step_sem, 1)
                eng.wait_ge(step_sem, base + 10)
            nc.gpsimd.tensor_tensor(n_b, neg_mean, rs, ALU.mult).then_inc(step_sem, 1)

        w3_in, w3_step = sem("w3_in"), sem("w3_step")
        xg_in = [sem(f"xg_in{b}") for b in range(B)]
        stats3, ln3_step, h3_ready = sem("stats3"), sem("ln3_step"), sem("h3_ready")
        ht_full, ht_hi_done, ht_lo_done = sem("ht_full"), sem("ht_hi_done"), sem("ht_lo_done")
        ring_full, ring_free = sem("ring_full"), sem("ring_free")
        v_copied, v_read = sem("v_copied"), sem("v_read")
        stage_hi, stage_lo = sem("stage_hi"), sem("stage_lo")
        out_stored = sem("out_stored")
        LN3_STEPS = 10

        def h3_of(b):
            return xg[1][:, 2 + b % 2] if b < GROUP else h3_late

        def h3_bank(b, h):
            return misc if h == 1 and b != 2 else pv_bank

        def flat(ap):
            return ap.rearrange("p k c -> p (k c)")

        block = ctx.enter_context(nc.Block())

        @block.sync
        def _(sp):
            sp.dma_start(xc[:, :, :], x[0].rearrange("(k p) c -> p k c", p=P)).then_inc(x_in, 16)
            for k in range(4):
                sp.dma_start(a_nat[:, 2 * k:2 * k + 2, :],
                             adj[2 * k * P:(2 * k + 2) * P, :].rearrange("(k p) n -> p k n", p=P)
                             ).then_inc(adj_in[k], 16)

            @for_batches
            def load_x(b):
                if known(b) and b == 0:
                    return
                wait(sp, *drained("L0w1", b - 1))
                sp.dma_start(xc[:, :, :], x[b:b + 1].rearrange("o (k p) c -> p (o k) c", p=P)
                             if known(b) else
                             x[bass.ds(b, 1)].rearrange("o (k p) c -> p (o k) c", p=P)).then_inc(x_in, 16)

            def one(dram, b):
                return (dram[b:b + 1] if known(b) else dram[bass.ds(b, 1)]).rearrange("o p n -> p (o n)")

            @for_batches
            def store_x1(b):
                wait(sp, *drained("L0w1", b))
                sp.dma_start(one(x1_dram, b), xa[:, :, :].rearrange("p k c -> p (k c)")).then_inc(x1_stored, 16)

            @for_batches
            def load_x1(b):
                wait(sp, x3_stored, 16 * b)
                wait(sp, x1_stored, 16 * (b + 1))
                sp.dma_start(xb[:, :, :].rearrange("p k c -> p (k c)"), one(x1_dram, b)).then_inc(x1_loaded, 16)

            @for_batches
            def store_x3(b):
                wait(sp, *drained("L2w1", b))
                sp.dma_start(one(x3_dram, b), xb[:, :, :].rearrange("p k c -> p (k c)")).then_inc(x3_stored, 16)

            def load_w3():
                wait(sp, *drained("L0w1", B - 1))
                sp.dma_start(w3_raw, W3).then_inc(w3_in, 16)

            def load_x3(b):
                wait(sp, w3_step, 6)
                wait(sp, x3_stored, 16 * (b + 1))
                if b < GROUP:
                    wait(sp, scored, T * B)
                else:
                    wait(sp, x3_stored, 16 * B)
                    wait(sp, ht_full, 2 * GROUP)
                sp.dma_start(xg[b // GROUP][:, b % GROUP].rearrange("p k c -> p (k c)"), one(x3_dram, b)
                             ).then_inc(xg_in[b], 16)

            def iteration(t):
                load_x(t + 3)
                store_x1(t + 2)
                store_x3(t - 1)
                load_x1(t)

            def drain():
                store_x3(B - 1)

            for t in range(FIRST, LOOP_FROM):
                iteration(t)
            with sp.Fori(LOOP_FROM, LOOP_TO) as t:
                iteration(t)
            for t in range(LOOP_TO, B - 1):
                iteration(t)
            load_w3()
            load_x3(0)
            load_x3(1)
            iteration(B - 1)
            load_x3(2)
            load_x3(3)
            drain()

            for b in range(GROUP, B):
                load_x3(b)
            for g in range(B // GROUP):
                for i in range(T):
                    wait(sp, ring_free, RING["S", g, STAGES - 1, i] + 1)
                    sp.dma_start(out[g * GROUP:(g + 1) * GROUP, i * P:(i + 1) * P, :].rearrange("b p c -> p b c"),
                                 xg[g][:, :, i, :]).then_inc(out_stored, 16)
            wait(sp, out_stored, (B // GROUP) * 16 * T)

        @block.gpsimd
        def _(pool):
            nc.gpsimd.memset(ident[:, :], 0.0).then_inc(ident_done, 1)
            nc.gpsimd.memset(neg_half[:, :], -0.5)
            nc.gpsimd.memset(slopes[:, :], SLOPE)
            pool.wait_ge(ident_done, 1)
            nc.gpsimd.affine_select(out=ident[:, :], in_=ident[:, :], compare_op=ALU.not_equal, fill=1.0,
                                    base=0, pattern=[[-1, P]], channel_multiplier=1).then_inc(ident_done, 1)
            def make_d():
                pool.wait_ge(rows_summed, T)
                nc.gpsimd.tensor_scalar(d_raw[:, :], d_raw[:, :], 1.0, None, ALU.add).then_inc(d_step, 1)
                pool.wait_ge(d_step, 1)
                nc.gpsimd.tensor_tensor(d_col[:, :], d_raw[:, :], neg_half[:, :], ALU.pow).then_inc(d_step, 1)
                pool.wait_ge(d_step, 2)

            @for_batches
            def coefficients(b, L):
                wait(pool, h_ready[L], b)
                norm_coefficients(pool, st[L], lt[L], rstd[L][:, :], nb[L][:, :], stats[L], b + 1,
                                  ln_step[L], LN_STEPS[L] * b, d_col[:, :] if L == 0 else None,
                                  make_d if known(b) and b == 0 and L == 0 else None)

            @for_batches
            def g_low(b):
                wait(pool, g_hi_done, b + 1)
                if exists(b - 1):
                    wait(pool, *filled("L0p1", b - 1))
                nc.gpsimd.tensor_tensor(g_lo[:, :, :], hn[:, :, :], g_hi[:, :, :].bitcast(f32),
                                        ALU.subtract).then_inc(g_lo_done, 1)

            @for_batches
            def bias_xc(b):
                wait(pool, h_ready[0], b + 1)
                nc.gpsimd.tensor_tensor(xc[:, :, :], xc[:, :, :],
                                        b0_row[:, :].unsqueeze(1).broadcast_to([P, T, C]),
                                        ALU.add).then_inc(xc_biased, 1)

            @for_batches
            def h1_low(b):
                wait(pool, h1_hi_done, b + 1)
                nc.gpsimd.tensor_tensor(h1_lo[:, :].rearrange("p (k c) -> p k c", c=C), h1s[:, :, 0:C],
                                        h1_hi[:, :].bitcast(f32).rearrange("p (k c) -> p k c", c=C),
                                        ALU.subtract).then_inc(h1_lo_done, 1)

            @for_batches
            def pair_coefficients(b, p):
                cols = slice(2 * p, 2 * p + 2)
                base = COEF_STEPS * b + PAIR_STEPS * p
                t0, t1, t2, t3, m = (ct[:, k, cols] for k in range(5))
                wait(pool, scored, T * b + 2 * p + 2)
                wait(pool, s_ready, b + 1)
                wait(pool, exps, T * (b - 1) + 2 * p + 2)
                wait(pool, coef_step, base)
                nc.gpsimd.tensor_tensor(t0, s_col[:, cols], dm[:, cols], ALU.add).then_inc(coef_step, 1)
                pool.wait_ge(coef_step, base + 1)
                nc.gpsimd.tensor_tensor(t2, t0, slopes[:, cols], ALU.mult).then_inc(coef_step, 1)
                nc.gpsimd.tensor_scalar(t1, t0, 0.0, 1.0 - SLOPE, ALU.max, ALU.mult).then_inc(coef_step, 1)
                pool.wait_ge(coef_step, base + 3)
                nc.gpsimd.tensor_tensor(m, t1, t2, ALU.add).then_inc(coef_step, 1)
                nc.gpsimd.tensor_tensor(t3, s_col[:, cols], slopes[:, cols], ALU.mult).then_inc(coef_step, 1)
                pool.wait_ge(coef_step, base + 5)
                nc.gpsimd.tensor_tensor(b1[:, cols], s_col[:, cols], m, ALU.subtract).then_inc(coef_step, 1)
                nc.gpsimd.tensor_tensor(b2[:, cols], t3, m, ALU.subtract).then_inc(coef_step, 1)

            @for_batches
            def u2_low(b):
                wait(pool, u2_hi, b + 1)
                nc.gpsimd.tensor_tensor(u_lo, hn[:, :, :].rearrange("p k c -> p (k c)"),
                                        u_hi.bitcast(f32), ALU.subtract).then_inc(u2_lo, 1)

            @for_batches
            def bias_xb(b):
                wait(pool, hw_read, b + 1)
                wait(pool, h_ready[2], b + 1)
                wait(pool, xb_biased, 2 * b)
                nc.gpsimd.tensor_tensor(c_row[:, :], hw_row[:, 1, :], bias2_row[:, :],
                                        ALU.add).then_inc(xb_biased, 1)
                pool.wait_ge(xb_biased, 2 * b + 1)
                nc.gpsimd.tensor_tensor(xb[:, :, :], xb[:, :, :],
                                        c_row[:, :].unsqueeze(1).broadcast_to([P, T, C]),
                                        ALU.add).then_inc(xb_biased, 1)

            def coefficients3(b):
                wait(pool, h3_ready, b)
                if b == 0:
                    wait(pool, h_ready[0], B)
                norm_coefficients(pool, st3, lt3, rstd3[:, :], nb3[:, :], stats3, b + 1,
                                  ln3_step, b * LN3_STEPS, None)

            def iteration(t):
                pair_coefficients(t + 1, 0)
                if known(t) and t == B - 1:
                    coefficients3(0)
                bias_xb(t - 1)
                coefficients(t + 3, 0)
                pair_coefficients(t + 1, 1)
                g_low(t + 3)
                bias_xc(t + 3)
                pair_coefficients(t + 1, 2)
                h1_low(t + 1)
                if known(t) and t == B - 1:
                    coefficients3(1)
                coefficients(t, 2)
                pair_coefficients(t + 1, 3)
                coefficients(t + 3, 1)
                if known(t) and t == B - 1:
                    coefficients3(2)
                u2_low(t)

            def drain():
                bias_xb(B - 1)
                coefficients3(3)

            for t in range(FIRST, LOOP_FROM):
                iteration(t)
            with pool.Fori(LOOP_FROM, LOOP_TO) as t:
                iteration(t)
            for t in range(LOOP_TO, LAST - 1):
                iteration(t)
            drain()

            for b in range(GROUP, B):
                coefficients3(b)

        @block.scalar
        def _(act):
            for dst, src in ((w_stage[:, 0, :], W0), (w_stage[:, 1, :], w1), (w2[:, :], W2),
                             (w_stage[:, 2, :], a_src.partition_broadcast(P)),
                             (w_stage[:, 3, :], a_dst.partition_broadcast(P)),
                             (b0_row[:, :], b0.partition_broadcast(P)),
                             (bias2_row[:, :], bias2.partition_broadcast(P)),
                             (gw_row[:, :], g_w.partition_broadcast(P)),
                             (gb_col, g_b.partition_broadcast(P))):
                act.dma_start(dst, src).then_inc(w_in, 16)

            for i in range(T):
                act.wait_ge(adj_in[i // 2], 16)
                if i >= 2:
                    act.wait_ge(rows_summed, i - 1)
                nc.scalar.activation(e2[:, i % 2, :], a_nat[:, i, :], ACT.Identity,
                                     accum_out=d_raw[:, i:i + 1]).then_inc(rows_summed, 1)
                act.wait_ge(at_tr, i + 1)
                nc.scalar.activation(at_hi[:, :, i * P:(i + 1) * P],
                                     tr[i % 2][:, :].rearrange("p (k i) -> p k i", i=P),
                                     ACT.Copy).then_inc(at_hi_done, 1)
            act.wait_ge(w0_tr, 1)
            nc.scalar.activation(w0t_hi[:, :], misc[:, 0:C], ACT.Copy).then_inc(w0_hi_done, 1)

            @for_batches
            def apply_norm(b, L):
                wait(act, ln_step[L], LN_STEPS[L] * (b + 1))
                src, dst = [(xc, hn), (xa, xa), (xb, hn)][L]
                if L == 0:
                    wait(act, g_lo_done, b)
                    wait(act, u2_lo, b - 3)
                    wait(act, sji_step, 2 * T * (b - 3))
                if L == 1:
                    wait(act, x1_stored, 16 * (b + 1))
                if L == 2:
                    wait(act, g_lo_done, min(b + 4, B) if known(b) else b + 4)
                for k in range(T):
                    last = nc.scalar.activation(dst[:, k, :], src[:, k, :], ACT.Relu,
                                                bias=nb[L][:, k:k + 1], scale=rstd[L][:, k:k + 1])
                last.then_inc(h_ready[L], 1)

            @for_batches
            def evacuate_hi(b, step, h, dst, done):
                if step == "hT" and exists(b - 3):
                    wait(act, *filled("L2p1", b - 3))
                    wait(act, moments_done, b - 2)
                k, n = side(f"{step}{h}", b)
                act.wait_ge(side_full[k], n + 1)
                nc.scalar.activation(dst[:, h * HALF:(h + 1) * HALF], side_bank[k][:, :],
                                     ACT.Copy).then_inc(done, 1)

            @for_batches
            def stage_h1(b, k):
                wait(act, h1_lo_done, b)
                wait(act, s_ready, b)
                bank, n = side(f"h1_{k}", b)
                tiles = H1_TILES[k]
                act.wait_ge(side_full[bank], n + 1)
                nc.scalar.activation(h1s[:, tiles[0]:tiles[-1] + 1, :],
                                     side_bank[bank][:, 0:len(tiles) * (C + 2)].rearrange("p (k c) -> p k c", c=C + 2),
                                     ACT.Copy).then_inc(side_free[bank], 1)

            @for_batches
            def split_h1(b):
                wait(act, pv_done, PAIRS * b)
                wait(act, *drained("h1_2", b))
                nc.scalar.activation(h1_hi[:, :].rearrange("p (k c) -> p k c", c=C), h1s[:, :, 0:C],
                                     ACT.Copy).then_inc(h1_hi_done, 1)

            @for_batches
            def spread_d(b, h):
                wait(act, scored, T * b)
                k, n = side(f"D{h}", b)
                act.wait_ge(side_full[k], n + 1)
                nc.scalar.activation(d_row[:, h * HALF:(h + 1) * HALF], side_bank[k][:, :],
                                     ACT.Copy).then_inc(side_free[k], 1)

            @for_batches
            def exponentials(b, i):
                n = T * b + i
                wait(act, coef_step, COEF_STEPS * b + PAIR_STEPS * (i // 2 + 1))
                wait(act, p_max, n - 1)
                nc.scalar.activation(e2[:, i % 2, :], tm[:, i % 4, :], ACT.Exp,
                                     bias=b2[:, i:i + 1], scale=SLOPE).then_inc(e2_done, 1)
                act.wait_ge(e2_done, n + 1)
                nc.scalar.activation(tm[:, i % 4, :], tm[:, i % 4, :], ACT.Exp,
                                     bias=b1[:, i:i + 1]).then_inc(exps, 1)

            @for_batches
            def pt_high(b, i):
                p, a = i // 2, i % 2
                wait(act, pv_done, PAIRS * b + p - 1)
                wait(act, p_tr, T * b + i + 1)
                nc.scalar.activation(pt_hi[:, p % 2, :, a * P:(a + 1) * P],
                                     tr[a][:, :].rearrange("p (k i) -> p k i", i=P),
                                     ACT.Copy).then_inc(p_hi, 1)

            @for_batches
            def evacuate_av(b, h):
                wait(act, pv_done, PAIRS * b + 2 * h + 2)
                if exists(b - 1):
                    wait(act, *filled(f"BT{h}", b - 1))
                nc.scalar.activation(avt[:, h * HALF:(h + 1) * HALF], pv_bank[:, :],
                                     ACT.Copy).then_inc(av_read, 1)

            @for_batches
            def read_moments(b):
                wait(act, moments_done, b + 1)
                wait(act, moments_turned, b)
                nc.scalar.activation(moments[0:3, :], misc[0:3, 0:2 * C], ACT.Copy).then_inc(moments_read, 1)

            @for_batches
            def spread_hw(b):
                wait(act, hw_full, b + 1)
                wait(act, hw_added, b)
                nc.scalar.activation(hw_row[:, :, :].rearrange("p k c -> p (k c)"), misc[:, 0:2 * C],
                                     ACT.Copy).then_inc(hw_read, 1)

            def apply_norm3(b):
                wait(act, ln3_step, (b + 1) * LN3_STEPS)
                wait(act, w3_step, 6)
                if b < GROUP:
                    wait(act, ht_full, 2 * (b - 1))
                else:
                    wait(act, ring_full, RING["V", b - 1, T - 1] + 1)
                for k in range(T):
                    last = nc.scalar.activation(h3_of(b)[:, k, :], xg[b // GROUP][:, b % GROUP, k, :], ACT.Relu,
                                                bias=nb3[:, k:k + 1], scale=rstd3[:, k:k + 1])
                last.then_inc(h3_ready, 1)

            def evacuate_h3(b, h):
                wait(act, ht_full, 2 * b + h + 1)
                if b > 0:
                    wait(act, ring_full, RING["V", b - 1, T - 1] + 1)
                nc.scalar.activation(ht_hi[:, h * HALF:(h + 1) * HALF], h3_bank(b, h)[:, :],
                                     ACT.Copy).then_inc(ht_hi_done, 1)

            def copy_v(b, i):
                n, (g, c) = RING["V", b, i], divmod(b, GROUP)
                wait(act, ring_full, n + 1)
                if g == 1:
                    wait(act, stage_lo, 2 * T)
                nc.scalar.activation(uu_hi[g][:, i, c * C:(c + 1) * C], ring[n % 4][:, 0:C], ACT.Copy)
                nc.scalar.activation(v[:, :, i, c, :], ring[n % 4][:, C:3 * C].rearrange("p (k c) -> p k c", c=C),
                                     ACT.Copy).then_inc(v_copied, 1)

            def stage_high(g, s, i):
                wait(act, ring_free, RING["S", g, s, i] + 1)
                nc.scalar.activation(uu_hi[(g + s + 1) % 2][:, i, :], flat(v[:, s, i, :, :]),
                                     ACT.Copy).then_inc(stage_hi, 1)

            def iteration(t):
                pt_high(t - 1, 7)
                apply_norm(t + 2, 0)
                evacuate_hi(t + 1, "hT", 0, u_hi, t_hi)
                evacuate_hi(t + 1, "hT", 1, u_hi, t_hi)
                pt_high(t, 0)
                exponentials(t, 2)
                exponentials(t, 3)
                evacuate_av(t - 1, 1)
                pt_high(t, 1)
                evacuate_hi(t + 2, "L0p", 0, ot_hi, o0_hi)
                split_h1(t)
                exponentials(t, 4)
                evacuate_hi(t + 2, "L0p", 1, ot_hi, o0_hi)
                exponentials(t, 5)
                stage_h1(t + 1, 0)
                pt_high(t, 2)
                stage_h1(t + 1, 1)
                pt_high(t, 3)
                spread_d(t + 1, 0)
                apply_norm(t - 1, 2)
                exponentials(t, 6)
                spread_d(t + 1, 1)
                stage_h1(t + 1, 2)
                exponentials(t, 7)
                read_moments(t - 1)
                pt_high(t, 4)
                apply_norm(t + 2, 1)
                pt_high(t, 5)
                evacuate_av(t, 0)
                evacuate_hi(t - 1, "L2p", 0, ot_hi, o2_hi)
                spread_hw(t - 1)
                exponentials(t + 1, 0)
                if known(t) and t == B - 1:
                    apply_norm3(0)
                evacuate_hi(t - 1, "L2p", 1, ot_hi, o2_hi)
                pt_high(t, 6)
                exponentials(t + 1, 1)

            def drain():
                pt_high(B - 1, 7)
                apply_norm3(1)
                evacuate_av(B - 1, 1)
                evacuate_h3(0, 0)
                evacuate_h3(0, 1)
                for i in range(T):
                    copy_v(0, i)
                evacuate_h3(1, 0)
                evacuate_h3(1, 1)
                apply_norm(B - 1, 2)
                for i in range(T):
                    copy_v(1, i)
                apply_norm3(2)
                read_moments(B - 1)
                evacuate_hi(B - 1, "L2p", 0, ot_hi, o2_hi)
                spread_hw(B - 1)
                evacuate_h3(2, 0)
                evacuate_h3(2, 1)
                evacuate_hi(B - 1, "L2p", 1, ot_hi, o2_hi)
                for i in range(T):
                    copy_v(2, i)
                apply_norm3(3)
                evacuate_h3(3, 0)
                evacuate_h3(3, 1)
                for i in range(T):
                    copy_v(3, i)

            for t in range(FIRST, LOOP_FROM):
                iteration(t)
            with act.Fori(LOOP_FROM, LOOP_TO) as t:
                iteration(t)
            for t in range(LOOP_TO, LAST - 1):
                iteration(t)
            drain()

            wait(act, x3_stored, 16 * B)
            for i in range(T):
                stage_high(0, 0, i)
            apply_norm3(GROUP)
            for i in range(T):
                stage_high(0, 1, i)
                if i == 1:
                    evacuate_h3(GROUP, 0)
                    evacuate_h3(GROUP, 1)
            for b in range(GROUP, B):
                for i in range(T):
                    copy_v(b, i)
                if b + 1 < B:
                    apply_norm3(b + 1)
                    evacuate_h3(b + 1, 0)
                    evacuate_h3(b + 1, 1)
            for s in range(STAGES - 1):
                for i in range(T):
                    stage_high(1, s, i)

        @block.vector
        def _(dve):
            def prepare_weights():
                dve.wait_ge(w_in, 9 * 16)
                dve.wait_ge(ident_done, 2)
                steps = [0]

                def w_step(ins):
                    steps[0] += 1
                    ins.then_inc(w_ready_dve, 1)

                w_step(nc.vector.tensor_copy(ident_r[:, :], ident[:, :]))
                w_step(nc.vector.tensor_copy(w1a_stage[:, 0:C], w_stage[:, 1, :]))
                w_step(nc.vector.tensor_tensor_reduce(junk[:, 0, :], w_stage[:, 1, :], w_stage[:, 2, :], 1.0, 0.0,
                                                      ALU.mult, ALU.add, w1a_stage[:, C:C + 1]))
                w_step(nc.vector.tensor_tensor_reduce(junk[:, 1, :], w_stage[:, 1, :], w_stage[:, 3, :], 1.0, 0.0,
                                                      ALU.mult, ALU.add, w1a_stage[:, C + 1:C + 2]))
                w_step(nc.vector.tensor_scalar(w_stage[:, 4, :], w2[:, :], gw_row[:, 2 * C:2 * C + 1], None, ALU.mult))
                w_step(nc.vector.memset(sv[:, :, :].bitcast(f32), 1.0))
                w_step(nc.vector.memset(pick[:, :, :], 1.0))
                w_step(nc.vector.memset(moments[:, :], 0.0))
                dve.wait_ge(w_ready_dve, 7)
                for k in (1, 2, 4, 5):
                    w_step(nc.vector.memset(pick[:, 0, k:k + 1], 0.0))
                for k in (0, 3):
                    w_step(nc.vector.tensor_copy(pick[:, 1, k:k + 1], gb_col))
                w_step(nc.vector.tensor_copy(w1_hi[:, :], w1a_stage))
                w_step(nc.vector.tensor_copy(w2r_hi[:, :], w_stage[:, 4, :]))
                dve.wait_ge(w_ready_dve, steps[0])
                w_step(nc.vector.tensor_tensor(w1_lo[:, :], w1a_stage, w1_hi[:, :].bitcast(f32), ALU.subtract))
                w_step(nc.vector.tensor_tensor(w2r_lo[:, :], w_stage[:, 4, :], w2r_hi[:, :].bitcast(f32), ALU.subtract))
                dve.wait_ge(w_ready_dve, steps[0])

            @for_batches
            def norm_stats(b, L):
                if L == 0:
                    wait(dve, x_in, 16 * (b + 1))
                elif L == 1:
                    wait(dve, *drained("L0w1", b))
                else:
                    wait(dve, *drained("BT1", b))
                wait(dve, ln_step[L], LN_STEPS[L] * b)
                src = [xc, xa, xb][L]
                for k in range(T):
                    last = nc.vector.bn_stats(st[L][:, k, :], src[:, k, :])
                last.then_inc(stats[L], 1)

            norm_stats(0, 0)
            for i in range(T):
                dve.wait_ge(adj_in[i // 2], 16)
                nc.vector.tensor_scalar(mask[:, i, :], a_nat[:, i, :], 0.0, MASKED, ALU.is_le,
                                        ALU.mult).then_inc(mask_done, 1)
                dve.wait_ge(at_hi_done, i + 1)
                nc.vector.tensor_tensor(at_lo[:, :, i * P:(i + 1) * P],
                                        tr[i % 2][:, :].rearrange("p (k i) -> p k i", i=P),
                                        at_hi[:, :, i * P:(i + 1) * P].bitcast(f32),
                                        ALU.subtract).then_inc(at_lo_done, 1)
                if i == HT:
                    prepare_weights()
            dve.wait_ge(w0_hi_done, 1)
            nc.vector.tensor_tensor(w0t_lo[:, :], misc[:, 0:C], w0t_hi[:, :].bitcast(f32),
                                    ALU.subtract).then_inc(w_ready, 1)

            @for_batches
            def split_g(b):
                wait(dve, h_ready[0], b + 1)
                if exists(b - 1):
                    wait(dve, *filled("L0p1", b - 1))
                nc.vector.tensor_copy(g_hi[:, :, :], hn[:, :, :]).then_inc(g_hi_done, 1)

            @for_batches
            def evacuate_lo(b, step, h, hi, lo, hi_done):
                k, n = side(f"{step}{h}", b)
                dve.wait_ge(hi_done, 2 * b + h + 1)
                cols = slice(h * HALF, (h + 1) * HALF)
                nc.vector.tensor_tensor(lo[:, cols], side_bank[k][:, :], hi[:, cols].bitcast(f32),
                                        ALU.subtract).then_inc(side_free[k], 1)

            @for_batches
            def residual0(b, h):
                k, n = side(f"L0w{h}", b)
                dve.wait_ge(side_full[k], n + 1)
                wait(dve, xc_biased, b + 1)
                if exists(b - 1):
                    wait(dve, *filled("hT1", b - 1))
                for q in range(HT):
                    i = h * HT + q
                    last = nc.vector.scalar_tensor_tensor(out=xa[:, i, :], in0=side_bank[k][:, q * P:(q + 1) * P],
                                                          scalar=d_col[:, i:i + 1], in1=xc[:, i, :],
                                                          op0=ALU.mult, op1=ALU.add)
                last.then_inc(side_free[k], 1)

            @for_batches
            def score(b, i):
                wait(dve, *drained("D1", b))
                wait(dve, p_tr, T * b + i - 3)
                nc.vector.memset(wait_cell[:, i % 4:i % 4 + 1], 0.0)
                nc.vector.tensor_tensor_reduce(tm[:, i % 4, :], mask[:, i, :], d_row[:, :], 1.0, -3.4e38,
                                               ALU.add, ALU.max, dm[:, i:i + 1]).then_inc(scored, 1)

            @for_batches
            def maximum(b, i):
                if i == 0:
                    wait(dve, rinv_done, b)
                wait(dve, exps, T * b + i + 1)
                nc.vector.scalar_tensor_tensor(out=tm[:, i % 4, :], in0=tm[:, i % 4, :], scalar=1.0,
                                               in1=e2[:, i % 2, :], op0=ALU.mult, op1=ALU.max,
                                               accum_out=rsum[:, i:i + 1]).then_inc(p_max, 1)

            @for_batches
            def pt_low(b, i):
                p, a = i // 2, i % 2
                wait(dve, p_hi, T * b + i + 1)
                cols = slice(a * P, (a + 1) * P)
                nc.vector.tensor_tensor(pt_lo[:, p % 2, :, cols],
                                        tr[a][:, :].rearrange("p (k i) -> p k i", i=P),
                                        pt_hi[:, p % 2, :, cols].bitcast(f32),
                                        ALU.subtract).then_inc(p_lo, 1)

            @for_batches
            def copy_s(b):
                wait(dve, *drained("h1_2", b))
                wait(dve, coef_step, COEF_STEPS * b)
                nc.vector.tensor_copy(s_col[:, :], h1s[:, :, C]).then_inc(s_ready, 1)

            @for_batches
            def invert_sums(b):
                wait(dve, p_max, T * (b + 1))
                if exists(b - 1):
                    wait(dve, *drained("BT1", b - 1))
                nc.vector.reciprocal(rinv[:, :], rsum[:, :]).then_inc(rinv_done, 1)

            @for_batches
            def residual1(b, h):
                k, n = side(f"BT{h}", b)
                dve.wait_ge(side_full[k], n + 1)
                wait(dve, x1_loaded, 16 * (b + 1))
                wait(dve, rinv_done, b + 1)
                for q in range(HT):
                    i = h * HT + q
                    last = nc.vector.scalar_tensor_tensor(out=xb[:, i, :], in0=side_bank[k][:, q * P:(q + 1) * P],
                                                          scalar=rinv[:, i:i + 1], in1=xb[:, i, :],
                                                          op0=ALU.mult, op1=ALU.add)
                last.then_inc(side_free[k], 1)

            @for_batches
            def split_u2(b):
                wait(dve, h_ready[2], b + 1)
                user = min(b + 2, B - 1) if known(b) else b + 2
                wait(dve, *filled("D1", user))
                wait(dve, *filled("h1_2", user))
                nc.vector.tensor_copy(u_hi, hn[:, :, :].rearrange("p k c -> p (k c)")).then_inc(u2_hi, 1)

            @for_batches
            def node_scores(b, w):
                wait(dve, h_ready[2], b + 1)
                if w == 0:
                    wait(dve, moments_done, b)
                else:
                    wait(dve, hw_added, b)
                for k in range(T):
                    wait(dve, sji_step, T * (2 * b + w) + max(k - 1, 0))
                    nc.vector.tensor_tensor_reduce(junk[:, k % 2, :], hn[:, k, :], gw_row[:, w * C:(w + 1) * C],
                                                   1.0, 0.0, ALU.mult, ALU.add,
                                                   sji[:, w, k:k + 1]).then_inc(sji_step, 1)
                if w == 0:
                    wait(dve, sji_step, T * (2 * b + 1))
                    nc.vector.tensor_copy(sv[:, :, 1], sji[:, 0, :]).then_inc(sv_done, 1)
                    wait(dve, sv_done, 2 * b + 1)
                    nc.vector.tensor_tensor(sv[:, :, 2], sji[:, 0, :], sv[:, :, 1].bitcast(f32),
                                            ALU.subtract).then_inc(sv_done, 1)

            @for_batches
            def combine_moments(b):
                wait(dve, moments_turned, b + 1)
                wait(dve, hw_full, b)
                for k in range(2):
                    wait(dve, hg_step, 2 * b + k)
                    nc.vector.tensor_tensor_reduce(junk_hg.rearrange("p (k w) -> p k w", w=3),
                                                   misc[:, 2 * C:4 * C].rearrange("p (k c) -> p k c", c=C)[:, :, 0:3],
                                                   pick[:, k, :].rearrange("p (k w) -> p k w", w=3), 1.0, 0.0,
                                                   ALU.mult, ALU.add, hg[:, k:k + 1]).then_inc(hg_step, 1)

            @for_batches
            def add_hw(b):
                wait(dve, xb_biased, 2 * b + 2)
                wait(dve, sji_step, 2 * T * (b + 1))
                for k in range(T):
                    last = nc.vector.scalar_tensor_tensor(out=xb[:, k, :], in0=hw_row[:, 0, :],
                                                          scalar=sji[:, 1, k:k + 1], in1=xb[:, k, :],
                                                          op0=ALU.mult, op1=ALU.add)
                last.then_inc(hw_added, 1)

            @for_batches
            def residual2(b, h):
                k, n = side(f"L2w{h}", b)
                dve.wait_ge(side_full[k], n + 1)
                wait(dve, hw_added, b + 1)
                rows = xb[:, h * HT:(h + 1) * HT, :].rearrange("p k c -> p (k c)")
                nc.vector.tensor_tensor(rows, side_bank[k][:, :], rows, ALU.add).then_inc(side_free[k], 1)

            def prepare_w3():
                dve.wait_ge(w3_in, 16)
                wait(dve, *filled("hT1", B - 1))
                wait(dve, *filled("L0p1", B - 1))
                for k in range(STAGES):
                    nc.vector.tensor_tensor(w3_sum[:, k, :], w3_raw[:, :, STAGES - k], w3_raw[:, :, 2 * STAGES - k],
                                            ALU.add).then_inc(w3_step, 1)
                nc.vector.tensor_copy(w3_sum[:, STAGES, :], w3_raw[:, :, 0]).then_inc(w3_step, 1)
                dve.wait_ge(w3_step, 4)
                nc.vector.tensor_copy(w3_hi[:, :], flat(w3_sum)).then_inc(w3_step, 1)
                dve.wait_ge(w3_step, 5)
                nc.vector.tensor_tensor(w3_lo[:, :], flat(w3_sum), w3_hi[:, :].bitcast(f32),
                                        ALU.subtract).then_inc(w3_step, 1)

            def norm_stats3(b):
                dve.wait_ge(xg_in[b], 16)
                if b == 0:
                    wait(dve, ln_step[0], LN_STEPS[0] * B)
                else:
                    wait(dve, ln3_step, b * LN3_STEPS)
                for k in range(T):
                    last = nc.vector.bn_stats(st3[:, k, :], xg[b // GROUP][:, b % GROUP, k, :])
                last.then_inc(stats3, 1)

            def split_h3(b, h):
                cols = slice(h * HALF, (h + 1) * HALF)
                wait(dve, ht_hi_done, 2 * b + h + 1)
                nc.vector.tensor_tensor(ht_lo[:, cols], h3_bank(b, h)[:, :], ht_hi[:, cols].bitcast(f32),
                                        ALU.subtract).then_inc(ht_lo_done, 1)

            def read_v(b, i):
                n, (g, c) = RING["V", b, i], divmod(b, GROUP)
                wait(dve, v_copied, b * T + i + 1)
                cols = slice(c * C, (c + 1) * C)
                nc.vector.tensor_tensor(uu_lo[g][:, i, cols], ring[n % 4][:, 0:C], uu_hi[g][:, i, cols].bitcast(f32),
                                        ALU.subtract).then_inc(v_read, 1)
                wait(dve, h3_ready, b + 1)
                nc.vector.tensor_tensor(xg[g][:, c, i, :], ring[n % 4][:, 3 * C:4 * C], xg[g][:, c, i, :],
                                        ALU.add).then_inc(ring_free, 1)

            def stage_sum(g, s, i):
                n = RING["S", g, s, i]
                wait(dve, ring_full, n + 1)
                if s == STAGES - 1:
                    nc.vector.tensor_tensor(xg[g][:, :, i, :], ring[n % 4][:, :].rearrange("p (b c) -> p b c", c=C),
                                            xg[g][:, :, i, :], ALU.add).then_inc(ring_free, 1)
                    return
                nc.vector.tensor_tensor(flat(v[:, s, i, :, :]), ring[n % 4][:, :], flat(v[:, s, i, :, :]),
                                        ALU.add).then_inc(ring_free, 1)
                k = (g + s + 1) % 2
                wait(dve, stage_hi, (2 * g + s) * T + i + 1)
                nc.vector.tensor_tensor(uu_lo[k][:, i, :], flat(v[:, s, i, :, :]), uu_hi[k][:, i, :].bitcast(f32),
                                        ALU.subtract).then_inc(stage_lo, 1)

            def iteration(t):
                score(t, 3)
                pt_low(t - 1, 7)
                maximum(t, 1)
                split_g(t + 2)
                evacuate_lo(t + 1, "hT", 0, u_hi, u_lo, t_hi)
                score(t, 4)
                evacuate_lo(t + 1, "hT", 1, u_hi, u_lo, t_hi)
                pt_low(t, 0)
                maximum(t, 2)
                score(t, 5)
                maximum(t, 3)
                residual1(t - 1, 0)
                evacuate_lo(t + 2, "L0p", 0, ot_hi, ot_lo, o0_hi)
                pt_low(t, 1)
                residual1(t - 1, 1)
                norm_stats(t - 1, 2)
                maximum(t, 4)
                evacuate_lo(t + 2, "L0p", 1, ot_hi, ot_lo, o0_hi)
                residual0(t + 2, 0)
                score(t, 6)
                residual0(t + 2, 1)
                score(t, 7)
                norm_stats(t + 2, 1)
                pt_low(t, 2)
                maximum(t, 5)
                pt_low(t, 3)
                if known(t) and t == B - 1:
                    prepare_w3()
                split_u2(t - 1)
                node_scores(t - 1, 0)
                score(t + 1, 0)
                maximum(t, 6)
                maximum(t, 7)
                score(t + 1, 1)
                copy_s(t + 1)
                if known(t) and t == B - 1:
                    norm_stats3(0)
                combine_moments(t - 1)
                invert_sums(t)
                pt_low(t, 4)
                if not (known(t) and t + 3 == 0):
                    norm_stats(t + 3, 0)
                pt_low(t, 5)
                evacuate_lo(t - 1, "L2p", 0, ot_hi, ot_lo, o2_hi)
                node_scores(t - 1, 1)
                maximum(t + 1, 0)
                if known(t) and t == B - 1:
                    norm_stats3(1)
                add_hw(t - 1)
                evacuate_lo(t - 1, "L2p", 1, ot_hi, ot_lo, o2_hi)
                residual2(t - 1, 0)
                score(t + 1, 2)
                residual2(t - 1, 1)
                pt_low(t, 6)

            def drain():
                pt_low(B - 1, 7)
                residual1(B - 1, 0)
                split_h3(0, 0)
                residual1(B - 1, 1)
                norm_stats(B - 1, 2)
                split_h3(0, 1)
                for i in range(T):
                    read_v(0, i)
                norm_stats3(2)
                split_h3(1, 0)
                split_h3(1, 1)
                split_u2(B - 1)
                node_scores(B - 1, 0)
                for i in range(T):
                    read_v(1, i)
                combine_moments(B - 1)
                evacuate_lo(B - 1, "L2p", 0, ot_hi, ot_lo, o2_hi)
                norm_stats3(3)
                node_scores(B - 1, 1)
                split_h3(2, 0)
                split_h3(2, 1)
                evacuate_lo(B - 1, "L2p", 1, ot_hi, ot_lo, o2_hi)
                add_hw(B - 1)
                for i in range(HT):
                    read_v(2, i)
                residual2(B - 1, 0)
                for i in range(HT, T):
                    read_v(2, i)
                residual2(B - 1, 1)
                split_h3(3, 0)
                split_h3(3, 1)
                for i in range(T):
                    read_v(3, i)

            for t in range(FIRST, LOOP_FROM):
                iteration(t)
            with dve.Fori(LOOP_FROM, LOOP_TO) as t:
                iteration(t)
            for t in range(LOOP_TO, LAST - 1):
                iteration(t)
            drain()

            for i in range(T):
                stage_sum(0, 0, i)
            norm_stats3(GROUP)
            for i in range(T):
                stage_sum(0, 1, i)
                if i == 1:
                    split_h3(GROUP, 0)
                    split_h3(GROUP, 1)
            for k in range(GROUP):
                b = GROUP + k
                if b + 1 < B:
                    norm_stats3(b + 1)
                stage_sum(0, 2, 2 * k)
                for i in range(T):
                    read_v(b, i)
                stage_sum(0, 2, 2 * k + 1)
                if b + 1 < B:
                    split_h3(b + 1, 0)
                    split_h3(b + 1, 1)
            for s in range(STAGES):
                for i in range(T):
                    stage_sum(1, s, i)

        @block.tensor
        def _(pe):
            def turn(dst, src):
                return nc.tensor.transpose(dst, src, ident[:, :])

            pe.wait_ge(ident_done, 2)
            for i in range(T):
                pe.wait_ge(adj_in[i // 2], 16)
                if i >= 2:
                    pe.wait_ge(at_lo_done, i - 1)
                for j in range(T):
                    last = turn(tr[i % 2][:, j * P:(j + 1) * P], a_nat[:, i, j * P:(j + 1) * P])
                last.then_inc(at_tr, 1)
            pe.wait_ge(w_in, 9 * 16)
            turn(misc[:, 0:C], w_stage[:, 0, :]).then_inc(w0_tr, 1)
            pe.wait_ge(w_ready, 1)
            pe.wait_ge(at_lo_done, T)

            def bank_of(step, b):
                k, n = side(step, b)
                return side_bank[k], side_full[k]

            def take(step, b):
                k, n = side(step, b)
                wait(pe, side_free[k], n)
                return bank_of(step, b)

            def propagate(bank, hi, lo, h, tiles, plus_identity):
                cols = slice(h * HALF, (h + 1) * HALF)
                for j in tiles:
                    nc.tensor.matmul(bank[:, :], hi(j), at_lo[:, j, cols], start=(j == 0), stop=False,
                                     skip_group_check=True)
                    if plus_identity and j // HT == h:
                        own = bank[:, (j % HT) * P:(j % HT + 1) * P]
                        for w in (hi, lo):
                            nc.tensor.matmul(own, w(j), ident_r[:, :], start=False, stop=False,
                                             skip_group_check=True)
                    nc.tensor.matmul(bank[:, :], hi(j), at_hi[:, j, cols], start=False, stop=False,
                                     skip_group_check=True)
                    last = nc.tensor.matmul(bank[:, :], lo(j), at_hi[:, j, cols], start=False,
                                            stop=(j == T - 1), skip_group_check=True)
                return last

            def tiles_of(tensor):
                return lambda j: tensor[:, j, :]

            def blocks_of(tensor):
                return lambda j: tensor[:, j * P:(j + 1) * P]

            PARTS = (range(0, HT), range(HT, T))

            def product(dst, l_hi, l_lo, r_hi, r_lo):
                nc.tensor.matmul(dst, l_hi, r_lo, start=True, stop=False)
                nc.tensor.matmul(dst, l_hi, r_hi, start=False, stop=False)
                return nc.tensor.matmul(dst, l_lo, r_hi, start=False, stop=True)

            @for_batches
            def l0_propagate(b, h, part):
                if part == 0:
                    wait(pe, g_lo_done, b + 1)
                    take(f"L0p{h}", b)
                bank, full = bank_of(f"L0p{h}", b)
                last = propagate(bank, tiles_of(g_hi), tiles_of(g_lo), h, PARTS[part], True)
                if part == 1:
                    last.then_inc(full, 1)

            @for_batches
            def rows_out(b, step, prop, h, r_hi, r_lo):
                wait(pe, *drained(f"{prop}{h}", b))
                bank, full = take(f"{step}{h}", b)
                for q in range(HT):
                    block_ = slice((h * HT + q) * P, (h * HT + q + 1) * P)
                    last = product(bank[:, q * P:(q + 1) * P], ot_hi[:, block_], ot_lo[:, block_], r_hi[:, :], r_lo[:, :])
                last.then_inc(full, 1)

            @for_batches
            def l1_turn(b, h):
                wait(pe, h_ready[1], b + 1)
                bank, full = take(f"hT{h}", b)
                for q in range(HT):
                    last = turn(bank[:, q * P:(q + 1) * P], xa[:, h * HT + q, :])
                last.then_inc(full, 1)

            @for_batches
            def l1_project(b, k):
                wait(pe, *drained(f"hT{H1_TILES[k][-1] // HT}", b))
                bank, full = take(f"h1_{k}", b)
                for q, i in enumerate(H1_TILES[k]):
                    last = product(bank[:, q * (C + 2):(q + 1) * (C + 2)], u_hi[:, i * P:(i + 1) * P],
                                   u_lo[:, i * P:(i + 1) * P], w1_hi[:, :], w1_lo[:, :])
                last.then_inc(full, 1)

            @for_batches
            def l1_rows(b, h):
                wait(pe, *drained(f"hT{h}", b))
                cols = slice(h * HALF, (h + 1) * HALF)
                bank, full = take(f"D{h}", b)
                product(bank[:, :], w1_hi[:, C + 1:C + 2].broadcast_to([P, P]),
                        w1_lo[:, C + 1:C + 2].broadcast_to([P, P]),
                        u_hi[:, cols], u_lo[:, cols]).then_inc(full, 1)

            @for_batches
            def turn_p(b, i):
                n = T * b + i
                wait(pe, p_max, n + 1)
                wait(pe, p_lo, n - 1)
                for j in range(T):
                    last = turn(tr[i % 2][:, j * P:(j + 1) * P], tm[:, i % 4, j * P:(j + 1) * P])
                last.then_inc(p_tr, 1)

            @for_batches
            def attend(b, p):
                wait(pe, p_lo, T * b + 2 * p + 2)
                wait(pe, h1_lo_done, b + 1)
                wait(pe, av_read, 2 * b + p // 2)
                dst = pv_bank[:, (p % 2) * 2 * P:(p % 2 + 1) * 2 * P]
                for j in range(T):
                    block_ = slice(j * P, (j + 1) * P)
                    for w, m in ((h1_hi, pt_lo), (h1_hi, pt_hi), (h1_lo, pt_hi)):
                        last = nc.tensor.matmul(dst, w[:, block_], m[:, p % 2, j, :],
                                                start=(j == 0 and w is h1_hi and m is pt_lo),
                                                stop=(j == T - 1 and w is h1_lo))
                last.then_inc(pv_done, 1)

            @for_batches
            def turn_back(b, h):
                wait(pe, av_read, 2 * b + h + 1)
                bank, full = take(f"BT{h}", b)
                for q in range(HT):
                    i = h * HT + q
                    last = turn(bank[:, q * P:(q + 1) * P], avt[:, i * P:(i + 1) * P])
                last.then_inc(full, 1)

            @for_batches
            def l2_moments(b):
                wait(pe, u2_lo, b + 1)
                wait(pe, sv_done, 2 * b + 2)
                wait(pe, hw_read, b)
                if known(b) and b == B - 1:
                    wait(pe, ht_lo_done, 4)
                for j in range(T):
                    last = nc.tensor.matmul(misc[0:3, 0:2 * C].rearrange("p (k c) -> p k c", c=C),
                                            sv[:, j, :], u[:, :, j * P:(j + 1) * P],
                                            start=(j == 0), stop=(j == T - 1))
                last.then_inc(moments_done, 1)

            @for_batches
            def turn_moments(b):
                wait(pe, moments_read, b + 1)
                wait(pe, hg_step, 2 * b)
                for k in range(2):
                    last = turn(misc[:, (2 + k) * C:(3 + k) * C], moments[:, k * C:(k + 1) * C])
                last.then_inc(moments_turned, 1)

            @for_batches
            def l2_propagate(b, h, part):
                if part == 0:
                    wait(pe, u2_lo, b + 1)
                    take(f"L2p{h}", b)
                bank, full = bank_of(f"L2p{h}", b)
                last = propagate(bank, blocks_of(u_hi), blocks_of(u_lo), h, PARTS[part], False)
                if part == 1:
                    last.then_inc(full, 1)

            @for_batches
            def l2_spread(b):
                wait(pe, hg_step, 2 * b + 2)
                for k in range(2):
                    last = nc.tensor.matmul(misc[:, k * C:(k + 1) * C], hg[:, k:k + 1].broadcast_to([P, P]), w2[:, :],
                                            start=True, stop=True)
                last.then_inc(hw_full, 1)

            def turn_h3(b, h):
                wait(pe, h3_ready, b + 1)
                bank = h3_bank(b, h)
                wait(pe, ht_lo_done, 2 * b + (h if b == 2 else 0))
                if b == 0:
                    wait(pe, av_read, 2 * B)
                if h == 1:
                    wait(pe, hw_read, B - 1 if b < 2 else B)
                for q in range(HT):
                    last = turn(bank[:, q * P:(q + 1) * P], h3_of(b)[:, h * HT + q, :])
                last.then_inc(ht_full, 1)

            def multiply_w3(b, i):
                n = RING["V", b, i]
                wait(pe, ht_lo_done, 2 * b + i // HT + 1)
                if n < 4:
                    wait(pe, p_lo, T * B)
                else:
                    wait(pe, ring_free, n - 3)
                product(ring[n % 4][:, :], ht_hi[:, i * P:(i + 1) * P], ht_lo[:, i * P:(i + 1) * P],
                        w3_hi[:, :], w3_lo[:, :]).then_inc(ring_full, 1)

            def stage(g, s, i):
                n = RING["S", g, s, i]
                hi, lo = uu_hi[(g + s) % 2], uu_lo[(g + s) % 2]
                wait(pe, ring_free, n - 3)
                if s == 0 and i == 0:
                    wait(pe, v_read, (g + 1) * GROUP * T)
                for j in range(T):
                    if i == 0 and s > 0:
                        wait(pe, stage_lo, (2 * g + s - 1) * T + j + 1)
                    for w, m in ((at_lo, hi), (at_hi, hi), (at_hi, lo)):
                        last = nc.tensor.matmul(ring[n % 4][:, :], w[:, j, i * P:(i + 1) * P], m[:, j, :],
                                                start=(j == 0 and w is at_lo), stop=(j == T - 1 and m is lo))
                last.then_inc(ring_full, 1)

            def iteration(t):
                turn_p(t, 0)
                attend(t - 1, 3)
                turn_p(t, 1)
                turn_back(t - 1, 0)
                l0_propagate(t + 2, 0, 0)
                l0_propagate(t + 2, 0, 1)
                l0_propagate(t + 2, 1, 0)
                turn_back(t - 1, 1)
                l0_propagate(t + 2, 1, 1)
                rows_out(t + 2, "L0w", "L0p", 0, w0t_hi, w0t_lo)
                turn_p(t, 2)
                rows_out(t + 2, "L0w", "L0p", 1, w0t_hi, w0t_lo)
                l1_project(t + 1, 0)
                turn_p(t, 3)
                l1_project(t + 1, 1)
                l1_rows(t + 1, 0)
                attend(t, 0)
                l1_rows(t + 1, 1)
                l1_project(t + 1, 2)
                turn_p(t, 4)
                attend(t, 1)
                turn_p(t, 5)
                l2_moments(t - 1)
                l2_propagate(t - 1, 0, 0)
                turn_moments(t - 1)
                l2_propagate(t - 1, 0, 1)
                l2_spread(t - 1)
                l2_propagate(t - 1, 1, 0)
                l2_propagate(t - 1, 1, 1)
                rows_out(t - 1, "L2w", "L2p", 0, w2r_hi, w2r_lo)
                turn_p(t, 6)
                rows_out(t - 1, "L2w", "L2p", 1, w2r_hi, w2r_lo)
                l1_turn(t + 2, 0)
                turn_p(t, 7)
                l1_turn(t + 2, 1)
                attend(t, 2)

            def drain():
                attend(B - 1, 3)
                turn_back(B - 1, 0)
                turn_back(B - 1, 1)
                turn_h3(0, 0)
                turn_h3(0, 1)
                for i in range(T):
                    multiply_w3(0, i)
                turn_h3(1, 0)
                turn_h3(1, 1)
                for i in range(T):
                    multiply_w3(1, i)
                l2_moments(B - 1)
                l2_propagate(B - 1, 0, 0)
                turn_moments(B - 1)
                l2_propagate(B - 1, 0, 1)
                l2_spread(B - 1)
                turn_h3(2, 0)
                l2_propagate(B - 1, 1, 0)
                turn_h3(2, 1)
                l2_propagate(B - 1, 1, 1)
                for i in range(HT):
                    multiply_w3(2, i)
                rows_out(B - 1, "L2w", "L2p", 0, w2r_hi, w2r_lo)
                for i in range(HT, T):
                    multiply_w3(2, i)
                rows_out(B - 1, "L2w", "L2p", 1, w2r_hi, w2r_lo)
                turn_h3(3, 0)
                turn_h3(3, 1)
                for i in range(T):
                    multiply_w3(3, i)

            for t in range(FIRST, LOOP_FROM):
                iteration(t)
            with pe.Fori(LOOP_FROM, LOOP_TO) as t:
                iteration(t)
            for t in range(LOOP_TO, LAST - 1):
                iteration(t)
            drain()

            for i in range(T):
                stage(0, 0, i)
            for i in range(T):
                stage(0, 1, i)
                if i == 1:
                    turn_h3(GROUP, 0)
                    turn_h3(GROUP, 1)
            for k in range(GROUP):
                b = GROUP + k
                stage(0, 2, 2 * k)
                for i in range(T):
                    multiply_w3(b, i)
                stage(0, 2, 2 * k + 1)
                if b + 1 < B:
                    turn_h3(b + 1, 0)
                    turn_h3(b + 1, 1)
            for s in range(STAGES):
                for i in range(T):
                    stage(1, s, i)


_INS = ["x", "adj", "L0_gnn_W", "L0_gnn_b", "L1_gnn_w", "L1_gnn_a_src", "L1_gnn_a_dst", "L2_gnn_g_w",
        "L2_gnn_g_b", "L2_gnn_weight", "L2_gnn_bias", "L3_gnn_weight_1"]


def kernel(**inputs):
    import numpy as _np
    import concourse.bacc as _bacc
    from concourse import mybir as _mybir
    from concourse.bass_utils import run_bass_kernel_spmd as _run

    nc = _bacc.Bacc("TRN2", target_bir_lowering=False, num_devices=1)
    arrays, args = {}, []
    for name in _INS:
        a = _np.ascontiguousarray(inputs[name])
        if a.ndim == 0:
            a = a.reshape(1)
        arrays[f"in_{name}"] = a
        args.append(nc.dram_tensor(f"in_{name}", a.shape, _mybir.dt.from_np(a.dtype), kind="ExternalInput").ap())
    args.append(nc.dram_tensor("out_0", (B, N, C), _mybir.dt.float32, kind="ExternalOutput").ap())
    build(nc, *args)
    r = _run(nc, [arrays], core_ids=[0])
    return r.results[0]["out_0"]
```
